# Optimizing a Trainium2 kernel written in Bass

```python
import numpy as np
import jax
import jax.numpy as jnp

def _softmax(x, axis=-1):
    return jax.nn.softmax(x, axis=axis)

def _gelu(x):
    return jax.nn.gelu(x, approximate=True)

def _silu(x):
    return jax.nn.silu(x)

def _sigmoid(x):
    return jax.nn.sigmoid(x)

def _layernorm(x, axis=-1, eps=1e-05):
    m = jnp.mean(x, axis=axis, keepdims=True)
    v = jnp.var(x, axis=axis, keepdims=True)
    return (x - m) / jnp.sqrt(v + eps)

def _scatter_add(tgt, idx, src, axis=0):
    return tgt.at[idx].add(src)

def _segment_sum(src, seg, n):
    return jax.ops.segment_sum(src, seg, n)
kernel_name = 'mk_dlrm_tower_d1_rec_r8_b32020'

def setup_inputs(seed: int=0):
    np.random.seed(seed)
    _w = jnp.asarray

    def _rec_inputs():
        import jax
        import jax.numpy as jnp
        _tk = jax.random.key(seed)
        ids = jnp.stack([jax.random.randint(jax.random.fold_in(_tk, 200 + f), (512,), 0, v, jnp.int32) for f, v in enumerate([1000, 125000, 1000, 12500, 12500, 12500, 1000, 12500, 1000, 1250, 125000, 1250, 1250, 1000, 1000, 1250, 1000, 1250, 125000, 1000, 1250, 1000, 12500, 1000, 1000, 1000])], axis=1)
        tbl_0 = 0.05 * jax.random.normal(jax.random.fold_in(_tk, 500 + 0), (1000, 64), jnp.float32)
        tbl_1 = 0.05 * jax.random.normal(jax.random.fold_in(_tk, 500 + 1), (125000, 64), jnp.float32)
        tbl_2 = 0.05 * jax.random.normal(jax.random.fold_in(_tk, 500 + 2), (1000, 64), jnp.float32)
        tbl_3 = 0.05 * jax.random.normal(jax.random.fold_in(_tk, 500 + 3), (12500, 64), jnp.float32)
        tbl_4 = 0.05 * jax.random.normal(jax.random.fold_in(_tk, 500 + 4), (12500, 64), jnp.float32)
        tbl_5 = 0.05 * jax.random.normal(jax.random.fold_in(_tk, 500 + 5), (12500, 64), jnp.float32)
        tbl_6 = 0.05 * jax.random.normal(jax.random.fold_in(_tk, 500 + 6), (1000, 64), jnp.float32)
        tbl_7 = 0.05 * jax.random.normal(jax.random.fold_in(_tk, 500 + 7), (12500, 64), jnp.float32)
        tbl_8 = 0.05 * jax.random.normal(jax.random.fold_in(_tk, 500 + 8), (1000, 64), jnp.float32)
        tbl_9 = 0.05 * jax.random.normal(jax.random.fold_in(_tk, 500 + 9), (1250, 64), jnp.float32)
        tbl_10 = 0.05 * jax.random.normal(jax.random.fold_in(_tk, 500 + 10), (125000, 64), jnp.float32)
        tbl_11 = 0.05 * jax.random.normal(jax.random.fold_in(_tk, 500 + 11), (1250, 64), jnp.float32)
        tbl_12 = 0.05 * jax.random.normal(jax.random.fold_in(_tk, 500 + 12), (1250, 64), jnp.float32)
        tbl_13 = 0.05 * jax.random.normal(jax.random.fold_in(_tk, 500 + 13), (1000, 64), jnp.float32)
        tbl_14 = 0.05 * jax.random.normal(jax.random.fold_in(_tk, 500 + 14), (1000, 64), jnp.float32)
        tbl_15 = 0.05 * jax.random.normal(jax.random.fold_in(_tk, 500 + 15), (1250, 64), jnp.float32)
        tbl_16 = 0.05 * jax.random.normal(jax.random.fold_in(_tk, 500 + 16), (1000, 64), jnp.float32)
        tbl_17 = 0.05 * jax.random.normal(jax.random.fold_in(_tk, 500 + 17), (1250, 64), jnp.float32)
        tbl_18 = 0.05 * jax.random.normal(jax.random.fold_in(_tk, 500 + 18), (125000, 64), jnp.float32)
        tbl_19 = 0.05 * jax.random.normal(jax.random.fold_in(_tk, 500 + 19), (1000, 64), jnp.float32)
        tbl_20 = 0.05 * jax.random.normal(jax.random.fold_in(_tk, 500 + 20), (1250, 64), jnp.float32)
        tbl_21 = 0.05 * jax.random.normal(jax.random.fold_in(_tk, 500 + 21), (1000, 64), jnp.float32)
        tbl_22 = 0.05 * jax.random.normal(jax.random.fold_in(_tk, 500 + 22), (12500, 64), jnp.float32)
        tbl_23 = 0.05 * jax.random.normal(jax.random.fold_in(_tk, 500 + 23), (1000, 64), jnp.float32)
        tbl_24 = 0.05 * jax.random.normal(jax.random.fold_in(_tk, 500 + 24), (1000, 64), jnp.float32)
        tbl_25 = 0.05 * jax.random.normal(jax.random.fold_in(_tk, 500 + 25), (1000, 64), jnp.float32)
        _rk = jax.random.fold_in(_tk, 7)
        r_dense_t = 7.22013e-05 + 1.00017 * jax.random.normal(jax.random.fold_in(_rk, 101), (512, 256), jnp.float32)
        W_top1 = 0.0360844 * jax.random.normal(jax.random.fold_in(_tk, 801), (768, 512), jnp.float32)
        W_top2 = 0.0441942 * jax.random.normal(jax.random.fold_in(_tk, 802), (512, 256), jnp.float32)
        W_top3 = 0.0625 * jax.random.normal(jax.random.fold_in(_tk, 803), (256, 1), jnp.float32)
        b_top1 = jnp.zeros((512,), jnp.float32)
        b_top2 = jnp.zeros((256,), jnp.float32)
        return (r_dense_t, ids, tbl_0, tbl_1, tbl_2, tbl_3, tbl_4, tbl_5, tbl_6, tbl_7, tbl_8, tbl_9, tbl_10, tbl_11, tbl_12, tbl_13, tbl_14, tbl_15, tbl_16, tbl_17, tbl_18, tbl_19, tbl_20, tbl_21, tbl_22, tbl_23, tbl_24, tbl_25, W_top1, b_top1, W_top2, b_top2, W_top3)
    r_dense_t, ids, tbl_0, tbl_1, tbl_2, tbl_3, tbl_4, tbl_5, tbl_6, tbl_7, tbl_8, tbl_9, tbl_10, tbl_11, tbl_12, tbl_13, tbl_14, tbl_15, tbl_16, tbl_17, tbl_18, tbl_19, tbl_20, tbl_21, tbl_22, tbl_23, tbl_24, tbl_25, W_top1, b_top1, W_top2, b_top2, W_top3 = _rec_inputs()

    def _L0_rec_setup():
        import jax, jax.numpy as jnp
        import numpy as np
        EPS = 1e-05
        NI = 33
        TRIL_I, TRIL_J = np.tril_indices(NI, k=-1)

        def layer_norm(x, g, b):
            m = jnp.mean(x, axis=-1, keepdims=True)
            v = jnp.mean(jnp.square(x - m), axis=-1, keepdims=True)
            return (x - m) * jax.lax.rsqrt(v + EPS) * g + b
        key = jax.random.key(seed)
        ks = jax.random.split(key, 8)
        B, D_DENSE, N_SP, D_SP = (4096, 256, 26, 64)
        E, PROJ, MAXD, NFLAT = (128, 32, 512, 528)
        dense_t = jax.random.normal(ks[0], (B, D_DENSE), dtype=jnp.float32)
        sparse_t = jax.random.normal(ks[1], (B, N_SP, D_SP), dtype=jnp.float32)
        Wd = jax.random.normal(ks[2], (E, D_DENSE), dtype=jnp.float32) / np.sqrt(D_DENSE)
        Ws = jax.random.normal(ks[3], (E, D_SP), dtype=jnp.float32) / np.sqrt(D_SP)
        Wsi = jax.random.normal(ks[4], (PROJ, N_SP), dtype=jnp.float32) / np.sqrt(N_SP)
        Wl = jax.random.normal(ks[5], (MAXD, NFLAT), dtype=jnp.float32) / np.sqrt(NFLAT)
        gd = jnp.ones((E,), jnp.float32)
        bd = jnp.zeros((E,), jnp.float32)
        gs = jnp.ones((E,), jnp.float32)
        bs = jnp.zeros((E,), jnp.float32)
        gsi = jnp.ones((PROJ,), jnp.float32)
        bsi = jnp.zeros((PROJ,), jnp.float32)
        gl = jnp.ones((MAXD,), jnp.float32)
        bl = jnp.zeros((MAXD,), jnp.float32)
        return {'dense_t': dense_t, 'sparse_t': sparse_t, 'Wd': Wd, 'gd': gd, 'bd': bd, 'Ws': Ws, 'gs': gs, 'bs': bs, 'Wsi': Wsi, 'gsi': gsi, 'bsi': bsi, 'Wl': Wl, 'gl': gl, 'bl': bl, 'dims_in_use': 384}
    _L0_rec_all = _L0_rec_setup()
    _L0_rec_in = {k: v for k, v in _L0_rec_all.items() if k in ('Wd', 'gd', 'bd', 'Ws', 'gs', 'bs', 'Wsi', 'gsi', 'bsi', 'Wl', 'gl', 'bl')}
    del _L0_rec_all
    return {'r_dense_t': r_dense_t, 'ids': ids, 'tbl_0': tbl_0, 'tbl_1': tbl_1, 'tbl_2': tbl_2, 'tbl_3': tbl_3, 'tbl_4': tbl_4, 'tbl_5': tbl_5, 'tbl_6': tbl_6, 'tbl_7': tbl_7, 'tbl_8': tbl_8, 'tbl_9': tbl_9, 'tbl_10': tbl_10, 'tbl_11': tbl_11, 'tbl_12': tbl_12, 'tbl_13': tbl_13, 'tbl_14': tbl_14, 'tbl_15': tbl_15, 'tbl_16': tbl_16, 'tbl_17': tbl_17, 'tbl_18': tbl_18, 'tbl_19': tbl_19, 'tbl_20': tbl_20, 'tbl_21': tbl_21, 'tbl_22': tbl_22, 'tbl_23': tbl_23, 'tbl_24': tbl_24, 'tbl_25': tbl_25, 'W_top1': W_top1, 'b_top1': b_top1, 'W_top2': W_top2, 'b_top2': b_top2, 'W_top3': W_top3, 'L0_rec_Wd': _L0_rec_in['Wd'], 'L0_rec_gd': _L0_rec_in['gd'], 'L0_rec_bd': _L0_rec_in['bd'], 'L0_rec_Ws': _L0_rec_in['Ws'], 'L0_rec_gs': _L0_rec_in['gs'], 'L0_rec_bs': _L0_rec_in['bs'], 'L0_rec_Wsi': _L0_rec_in['Wsi'], 'L0_rec_gsi': _L0_rec_in['gsi'], 'L0_rec_bsi': _L0_rec_in['bsi'], 'L0_rec_Wl': _L0_rec_in['Wl'], 'L0_rec_gl': _L0_rec_in['gl'], 'L0_rec_bl': _L0_rec_in['bl']}

def reference(r_dense_t, ids, tbl_0, tbl_1, tbl_2, tbl_3, tbl_4, tbl_5, tbl_6, tbl_7, tbl_8, tbl_9, tbl_10, tbl_11, tbl_12, tbl_13, tbl_14, tbl_15, tbl_16, tbl_17, tbl_18, tbl_19, tbl_20, tbl_21, tbl_22, tbl_23, tbl_24, tbl_25, W_top1, b_top1, W_top2, b_top2, W_top3, L0_rec_Wd, L0_rec_gd, L0_rec_bd, L0_rec_Ws, L0_rec_gs, L0_rec_bs, L0_rec_Wsi, L0_rec_gsi, L0_rec_bsi, L0_rec_Wl, L0_rec_gl, L0_rec_bl):
    import jax
    import jax.numpy as jnp

    def _L0_rec_ref(dense_t, sparse_t, Wd, gd, bd, Ws, gs, bs, Wsi, gsi, bsi, Wl, gl, bl, dims_in_use):
        import jax, jax.numpy as jnp
        import numpy as np
        EPS = 1e-05
        NI = 33
        TRIL_I, TRIL_J = np.tril_indices(NI, k=-1)

        def layer_norm(x, g, b):
            m = jnp.mean(x, axis=-1, keepdims=True)
            v = jnp.mean(jnp.square(x - m), axis=-1, keepdims=True)
            return (x - m) * jax.lax.rsqrt(v + EPS) * g + b
        x = layer_norm(dense_t @ Wd.T, gd, bd)
        y = layer_norm(jnp.einsum('bnd,ed->bne', sparse_t, Ws), gs, bs)
        y = jnp.einsum('bne,pn->bep', y, Wsi)
        y = layer_norm(y, gsi, bsi)
        y = jnp.swapaxes(y, 1, 2)
        T = jnp.concatenate([x[:, None, :], y], axis=1)
        Z = jnp.einsum('bnd,bmd->bnm', T, T)
        Zflat = Z[:, TRIL_I, TRIL_J]
        out = layer_norm(Zflat @ Wl.T, gl, bl)
        maxd = out.shape[-1]
        mask = (jnp.arange(maxd) < dims_in_use).astype(out.dtype)
        return out * mask
    e = jnp.stack([tbl_0[ids[:, 0]], tbl_1[ids[:, 1]], tbl_2[ids[:, 2]], tbl_3[ids[:, 3]], tbl_4[ids[:, 4]], tbl_5[ids[:, 5]], tbl_6[ids[:, 6]], tbl_7[ids[:, 7]], tbl_8[ids[:, 8]], tbl_9[ids[:, 9]], tbl_10[ids[:, 10]], tbl_11[ids[:, 11]], tbl_12[ids[:, 12]], tbl_13[ids[:, 13]], tbl_14[ids[:, 14]], tbl_15[ids[:, 15]], tbl_16[ids[:, 16]], tbl_17[ids[:, 17]], tbl_18[ids[:, 18]], tbl_19[ids[:, 19]], tbl_20[ids[:, 20]], tbl_21[ids[:, 21]], tbl_22[ids[:, 22]], tbl_23[ids[:, 23]], tbl_24[ids[:, 24]], tbl_25[ids[:, 25]]], axis=1)
    z = _L0_rec_ref(r_dense_t, e, L0_rec_Wd, L0_rec_gd, L0_rec_bd, L0_rec_Ws, L0_rec_gs, L0_rec_bs, L0_rec_Wsi, L0_rec_gsi, L0_rec_bsi, L0_rec_Wl, L0_rec_gl, L0_rec_bl, 384)
    z = z.reshape(z.shape[0], -1)
    h = jnp.concatenate([z, r_dense_t], axis=1)
    h = jnp.maximum(h @ W_top1 + b_top1, 0.0)
    h = jnp.maximum(h @ W_top2 + b_top2, 0.0)
    y = h @ W_top3
    return y

_drawn_inputs = setup_inputs


def setup_inputs(seed=0):
    import zlib

    import numpy as np

    out = dict(_drawn_inputs(seed))
    spreads = {'b_top1': (0.0, 0.1),
     'b_top2': (0.0, 0.1),
     'L0_rec_gd': (1.0, 0.6),
     'L0_rec_bd': (0.0, 0.8),
     'L0_rec_gs': (1.0, 0.6),
     'L0_rec_bs': (0.0, 0.1),
     'L0_rec_gsi': (1.0, 0.2),
     'L0_rec_bsi': (0.0, 0.1),
     'L0_rec_gl': (1.0, 0.2),
     'L0_rec_bl': (0.0, 0.1)}
    factors = {}
    for name, (base, spread) in spreads.items():
        noise = np.random.default_rng([zlib.crc32(name.encode()), seed]).standard_normal(out[name].shape)
        drawn = base * np.exp(spread * noise) if base else spread * noise
        out[name] = jnp.asarray(drawn.astype(out[name].dtype))
    for name, factor in factors.items():
        out[name] = (out[name] * factor).astype(out[name].dtype)
    return out
```

```python
from contextlib import ExitStack

import numpy as np

import concourse.bass as bass
from concourse import mybir

ALU = mybir.AluOpType
ACT = mybir.ActivationFunctionType
AX = mybir.AxisListType
F32 = mybir.dt.float32
I32 = mybir.dt.int32

P = 128
VOCAB = [1000, 125000, 1000, 12500, 12500, 12500, 1000, 12500, 1000, 1250, 125000, 1250, 1250, 1000,
         1000, 1250, 1000, 1250, 125000, 1000, 1250, 1000, 12500, 1000, 1000, 1000]
NF = len(VOCAB)
D = 64
EW = 128
PR = 32
B = 512
CHUNKS = B // P
HALF = P // 2
TILES = HALF * NF // P
QUARTERS = 4
QB = HALF // QUARTERS
SLOTS = CHUNKS * QUARTERS
SPAN = 6
MAXD = 512
USED = 384
DENSE = 256
H1 = 512
H2 = 256
KZ = PR * PR // P
KU = USED // P
KD = DENSE // P
EPS = 1e-5


def first_sample(t):
    return P * t // NF


def tiles_of(q):
    end = [-(-(q1 + 1) * QB * NF // P) for q1 in range(QUARTERS)]
    begin = end[q - 1] if q else 0
    return begin, end[q] - begin


def mix_parts(q):
    parts = []
    for t in range(TILES):
        lo = max(q * QB, first_sample(t))
        hi = min((q + 1) * QB, (P * (t + 1) - 1) // NF + 1)
        if lo < hi:
            parts.append((t, lo - first_sample(t), lo - q * QB, hi - lo))
    return parts


PACK = {}
for _name, _width in (("eye", P), ("ws", EW), ("wsi", PR), ("gsi", PR), ("bsi", PR), ("gs", 1), ("gd", 1), ("bd", 1),
                      ("gl", USED // P), ("bl", USED // P), ("b1", H1 // P), ("b2", H2 // P), ("w3", H2 // P)):
    _at = max([end for _, end in PACK.values()], default=0)
    PACK[_name] = (_at, _at + _width)
PACKED = max(end for _, end in PACK.values())


def tower(nc, table, ids, offs, small, mixw, dense_t, wd_t, wl, w1, w2, out):
    with ExitStack() as ctx:
        def sb(name, shape, dt=F32):
            return ctx.enter_context(nc.sbuf_tensor(name, shape, dt))

        def psum(name, shape):
            return ctx.enter_context(nc.psum_tensor(name, shape, F32))

        def sem(name):
            return ctx.enter_context(nc.semaphore(name))

        turn_ps = psum("turn_ps", [P, 512])
        quad_ps = psum("quad_ps", [P, 512])
        mix_ps = psum("mix_ps", [P, 512])
        dots_ps = psum("dots_ps", [P, 512])
        proj_ps = psum("proj_ps", [P, 2, 2, 512])

        ids_sb = sb("ids_sb", [P, CHUNKS * TILES * 2], I32)
        offs_sb = sb("offs_sb", [P, CHUNKS * TILES * 2], I32)
        rows_sb = sb("rows_sb", [P, CHUNKS * TILES * 2], I32)
        e_rows = sb("e_rows", [P, TILES, 2 * D])
        e_unit = sb("e_unit", [P, TILES, 2 * D])
        e_cols = sb("e_cols", [P, 2, 4 * P])
        e_prod = sb("e_prod", [P, 4 * 2, D])
        var_n = sb("var_n", [P, 8])
        std_n = sb("std_n", [P, 8])
        rstd_n = sb("rstd_n", [P, 8])
        f_sb = sb("f_sb", [D + 1, 2, 2, 512])
        y_sq = sb("y_sq", [P, 2 * QB, PR])
        var_p = sb("var_p", [P, 2 * QB])
        std_p = sb("std_p", [P, 2 * QB])
        rstd_p = sb("rstd_p", [P, 2 * QB])
        y_a = sb("y_a", [P, 2 * QB, PR])
        y_b = sb("y_b", [P, 2 * QB, PR])
        feats = sb("feats", [P, 2, 2 * QB, PR + 1])
        z_mine = sb("z_mine", [P, CHUNKS, PR, PR])
        z_pairs = sb("z_pairs", [P, CHUNKS, 4, KZ, PR])

        small_sb = sb("small_sb", [P, PACKED])
        eye_sb, ws_sb, wsi_sb, gsi_sb, bsi_sb, gs_sb, gd_sb, bd_sb, gl_sb, bl_sb, b1_sb, b2_sb, w3_sb = (
            small_sb[:, begin:end] for begin, end in PACK.values())
        ones = sb("ones", [P, P])
        eps = sb("eps", [P, 1])
        mixw_sb = sb("mixw_sb", [P, TILES * SPAN, PR])
        mixw_mean = sb("mixw_mean", [P, TILES * SPAN])
        mixw_c = sb("mixw_c", [P, TILES * SPAN, PR])
        wsi_mean = sb("wsi_mean", [NF, 1])
        wsi_c = sb("wsi_c", [NF, PR])
        ws_mean = sb("ws_mean", [D, 1])
        ws_c = sb("ws_c", [D, EW])
        ws_rows = sb("ws_rows", [EW, 2, D])
        ws_grows = sb("ws_grows", [EW, D])
        gram = sb("gram", [P, P])
        proj_w = sb("proj_w", [D + 1, EW])
        dense_sb = sb("dense_sb", [P, KD, B])
        wd_sb = sb("wd_sb", [P, KD, EW])
        wd_mean = sb("wd_mean", [P, KD])
        wd_c = sb("wd_c", [P, KD, EW])
        x_sq = sb("x_sq", [P, B])
        x_std = sb("x_std", [P, B])
        x_rstd = sb("x_rstd", [P, B])
        x_unit = sb("x_unit", [P, B])
        x_sb = sb("x_sb", [P, B])
        wl_sb = sb("wl_sb", [P, KZ, MAXD])
        wl_mean = sb("wl_mean", [P, KZ])
        wl_c = sb("wl_c", [P, KZ, MAXD])
        w1_sb = sb("w1_sb", [P, KU + KD, H1])
        w1_g = sb("w1_g", [P, KU, H1])
        b1_all = sb("b1_all", [P, H1 // P])
        w2_sb = sb("w2_sb", [P, H1 // P, H2])
        o_sq = sb("o_sq", [P, MAXD // P, B])
        o_std = sb("o_std", [P, B])
        o_rstd = sb("o_rstd", [P, B])
        z_unit = sb("z_unit", [P, KU, B])
        h1_sb = sb("h1_sb", [P, H1 // P, B])
        h2_sb = sb("h2_sb", [P, H2 // P, B])
        y_out = sb("y_out", [1, B])

        ids_in, small_in, mixw_in, dense_in = sem("ids_in"), sem("small_in"), sem("mixw_in"), sem("dense_in")
        wl_in, top_in, out_done = sem("wl_in"), sem("top_in"), sem("out_done")
        gathered = [sem(f"gathered{q}") for q in range(QUARTERS)]
        rows_ready = sem("rows_ready")
        consts = sem("consts")
        prep_dve, prep_pe, prep_act = sem("prep_dve"), sem("prep_pe"), sem("prep_act")
        turned, cols_ready, quad_done, var_ready, std_ready, unit_ready = (
            sem(n) for n in ("turned", "cols_ready", "quad_done", "var_ready", "std_ready", "unit_ready"))
        mixed, f_ready, projected, sq_ready, ssq_ready, stdp_ready = (
            sem(n) for n in ("mixed", "f_ready", "projected", "sq_ready", "ssq_ready", "stdp_ready"))
        y_ready, x_placed, dotted, z_saved, z_moved = (
            sem(n) for n in ("y_ready", "x_placed", "dotted", "z_saved", "z_moved"))
        chain = sem("chain")
        prod_done, rstdn_done, rstdp_done, y_unit, y_gained = (
            sem(n) for n in ("prod_done", "rstdn_done", "rstdp_done", "y_unit", "y_gained"))
        o_done, osq_done, ovar_done, ostd_done, zu_done = (
            sem(n) for n in ("o_done", "osq_done", "ovar_done", "ostd_done", "zu_done"))
        h1_done, h1_ready, h2_done, h2_ready, top_done, y_done = (
            sem(n) for n in ("h1_done", "h1_ready", "h2_done", "h2_ready", "top_done", "y_done"))

        block = ctx.enter_context(nc.Block())

        def slots(eng, stages, once=None):
            latest = max(late for late, _ in stages)

            def slot(chunk, q, s=None):
                for late, stage in stages:
                    if s is None or 0 <= s - late < SLOTS:
                        stage(chunk + (q - late) // QUARTERS, (q - late) % QUARTERS)

            for q in range(QUARTERS):
                slot(0, q, q)
                if once and q == 2:
                    once()
            with eng.Fori(1, CHUNKS) as chunk:
                for q in range(QUARTERS):
                    slot(chunk, q)
            for s in range(SLOTS, SLOTS + latest):
                slot(s // QUARTERS, s % QUARTERS, s)

        def wait(eng, semaphore, count):
            if not isinstance(count, int) or count > 0:
                eng.wait_ge(semaphore, count)

        @block.sync
        def _(sp):
            sp.dma_start(ids_sb[:], ids).then_inc(ids_in, 16)
            sp.dma_start(offs_sb[:], offs).then_inc(ids_in, 16)
            sp.dma_start(small_sb[:], small).then_inc(small_in, 16)
            sp.dma_start(wd_sb[:], wd_t).then_inc(dense_in, 16)
            sp.dma_start(dense_sb[:], dense_t).then_inc(dense_in, 16)
            sp.dma_start(mixw_sb[:], mixw).then_inc(mixw_in, 16)
            sp.dma_start(wl_sb[:], wl).then_inc(wl_in, 16)
            sp.dma_start(w1_sb[:], w1).then_inc(top_in, 16)
            sp.dma_start(w2_sb[:], w2).then_inc(top_in, 16)
            with sp.Fori(0, CHUNKS) as chunk:
                sp.wait_ge(z_saved, chunk * QUARTERS + QUARTERS)
                for k in range(4):
                    for c in range(4):
                        sp.dma_start(
                            z_pairs[PR * c:PR * (c + 1), bass.ds(chunk, 1), k, :, :],
                            z_mine[PR * k:PR * (k + 1), bass.ds(chunk, 1), KZ * c:KZ * (c + 1), :],
                        ).then_inc(z_moved, 16)
            sp.wait_ge(y_done, 1)
            sp.dma_start(out, y_out[:]).then_inc(out_done, 16)
            sp.wait_ge(out_done, 16)

        @block.gpsimd
        def _(pool):
            pool.memset(ones[:], 1.0).then_inc(consts, 1)
            pool.memset(eps[:], EPS).then_inc(consts, 1)
            pool.memset(gram[:], 0.0).then_inc(consts, 1)
            pool.wait_ge(rows_ready, 1)
            for chunk in range(CHUNKS):
                for q in range(QUARTERS):
                    wait(pool, unit_ready, QUARTERS * (chunk - 1) + q + 1)
                    t0, nt = tiles_of(q)
                    for t in range(t0, t0 + nt):
                        for ab in range(2):
                            col = (chunk * TILES + t) * 2 + ab
                            pool.indirect_dma_start(
                                out=e_rows[:, t, D * ab:D * (ab + 1)], out_offset=None, in_=table,
                                in_offset=bass.IndirectOffsetOnAxis(ap=rows_sb[:, col:col + 1], axis=0),
                            ).then_inc(gathered[q], 16)

        @block.tensor
        def _(pe):
            pe.wait_ge(small_in, 16)
            pe.wait_ge(consts, 3)
            pe.wait_ge(prep_dve, 2)
            pe.matmul(quad_ps[:, 0:PR], ones[0:NF, :], wsi_c[:], start=True, stop=True).then_inc(prep_pe, 1)
            pe.transpose(turn_ps[:, 0:D], ws_c[:], eye_sb[0:D, 0:D]).then_inc(prep_pe, 1)
            pe.wait_ge(prep_act, 2)
            pe.matmul(mix_ps[:, 0:D], ws_rows[:].rearrange("p a d -> p (a d)"), ws_rows[:, 0, :], start=True,
                      stop=True).then_inc(prep_pe, 1)
            pe.wait_ge(prep_act, 3)
            pe.transpose(dots_ps[0:D, 0:EW], ws_grows[:], eye_sb).then_inc(prep_pe, 1)
            pe.wait_ge(dense_in, 32)
            pe.wait_ge(prep_dve, 4)
            for j in range(KD):
                mm = pe.matmul(proj_ps[:, 0, 0, :], wd_c[:, j, :], dense_sb[:, j, :], start=(j == 0), stop=(j == KD - 1))
            mm.then_inc(prep_pe, 1)
            pe.wait_ge(prep_act, 4)
            pe.matmul(proj_ps[:, 0, 1, :], ones[:], x_sq[:], start=True, stop=True).then_inc(prep_pe, 1)
            pe.wait_ge(prep_act, 7)
            pe.wait_ge(prep_dve, 8)

            def turn(chunk, q):
                t0, nt = tiles_of(q)
                s = chunk * QUARTERS + q
                pe.wait_ge(gathered[q], chunk * (32 * nt) + 32 * nt)
                wait(pe, cols_ready, s)
                for t in range(nt):
                    mm = pe.transpose(turn_ps[:, P * t:P * (t + 1)], e_rows[:, t0 + t, :], eye_sb)
                mm.then_inc(turned, 1)

            def mix(chunk, q):
                s = chunk * QUARTERS + q
                pe.wait_ge(unit_ready, s + 1)
                wait(pe, f_ready, 2 * s)
                for n, (t, lo, at, number) in enumerate(mix_parts(q)):
                    mm = pe.matmul(mix_ps[:, PR * at:PR * (at + number)], e_unit[:, t, :],
                                   mixw_c[:, SPAN * t + lo:SPAN * t + lo + number, :].rearrange("k b p -> k (b p)"),
                                   start=(n == 0), stop=(n == len(mix_parts(q)) - 1), skip_group_check=True)
                mm.then_inc(mixed, 1)

            def quad(chunk, q):
                _, nt = tiles_of(q)
                s = chunk * QUARTERS + q
                pe.wait_ge(cols_ready, s + 1)
                wait(pe, var_ready, s)
                for t in range(nt):
                    mm = pe.matmul(quad_ps[:, P * t:P * (t + 1)], e_cols[:, q % 2, P * t:P * (t + 1)], gram[:],
                                   start=True, stop=True)
                mm.then_inc(quad_done, 1)

            def dots(chunk, q):
                s = chunk * QUARTERS + q
                pe.wait_ge(y_ready, s + 1)
                pe.wait_ge(x_placed, s + 1)
                wait(pe, z_saved, s)
                for g in range(2 * QB // 4):
                    for k in range(4):
                        f = feats[:, q % 2, 4 * g + k, :]
                        mm = pe.matmul(dots_ps[PR * k:PR * (k + 1), PR * g:PR * (g + 1)], f[:, 1:PR + 1], f[:, 0:PR],
                                       start=True, stop=True)
                mm.then_inc(dotted, 1)

            def project(chunk, q):
                s = chunk * QUARTERS + q
                wait(pe, y_ready, s - 1)
                for ab in range(2):
                    pe.wait_ge(f_ready, 2 * s + ab + 1)
                    pe.matmul(proj_ps[:, q % 2, ab, :], proj_w[:], f_sb[:, q % 2, ab, :], start=True,
                              stop=True).then_inc(projected, 1)

            slots(pe, [(0, turn), (1, mix), (0, quad), (3, dots), (1, project)])

            pe.wait_ge(z_saved, SLOTS)
            pe.wait_ge(y_ready, SLOTS)
            pe.wait_ge(top_in, 32)
            pe.wait_ge(prep_act, 7)
            for j in range(H1 // P):
                for c in range(KU):
                    mm = pe.matmul(dots_ps[:, j:j + 1], w1_sb[:, c, P * j:P * (j + 1)], bl_sb[:, c:c + 1],
                                   start=(c == 0), stop=(c == KU - 1))
            mm.then_inc(prep_pe, 1)
            pe.wait_ge(z_moved, 16 * 16 * CHUNKS)
            o_ps = [proj_ps[:, j // 2, j % 2, :] for j in range(MAXD // P)]
            for j in range(MAXD // P):
                for c in range(KZ):
                    mm = pe.matmul(o_ps[j], wl_c[:, c, P * j:P * (j + 1)],
                                   z_pairs[:, :, :, c, :].rearrange("p s k g -> p (s k) g"),
                                   start=(c == 0), stop=(c == KZ - 1))
                mm.then_inc(o_done, 1)
            for j in range(MAXD // P):
                pe.wait_ge(osq_done, j + 1)
                mm = pe.matmul(mix_ps[:], ones[:], o_sq[:, j, :], start=(j == 0), stop=(j == MAXD // P - 1))
            mm.then_inc(ovar_done, 1)
            pe.wait_ge(prep_dve, 10)
            h1_ps = [turn_ps[:], quad_ps[:], dots_ps[:], mix_ps[:]]
            for j in range(H1 // P):
                if j == 3:
                    pe.wait_ge(ostd_done, 1)
                for c in range(KD):
                    pe.matmul(h1_ps[j], w1_sb[:, KU + c, P * j:P * (j + 1)], dense_sb[:, c, :], start=(c == 0),
                              stop=False)
                for c in range(KU):
                    pe.wait_ge(zu_done, c + 1)
                    mm = pe.matmul(h1_ps[j], w1_g[:, c, P * j:P * (j + 1)], z_unit[:, c, :], start=False,
                                   stop=(c == KU - 1))
                mm.then_inc(h1_done, 1)
            h2_ps = o_ps[0:2]
            for c in range(H1 // P):
                pe.wait_ge(h1_ready, c + 1)
                for j in range(H2 // P):
                    mm = pe.matmul(h2_ps[j], w2_sb[:, c, P * j:P * (j + 1)], h1_sb[:, c, :], start=(c == 0),
                                   stop=(c == H1 // P - 1), skip_group_check=True)
                    if c == H1 // P - 1:
                        mm.then_inc(h2_done, 1)
            for c in range(H2 // P):
                pe.wait_ge(h2_ready, c + 1)
                mm = pe.matmul(o_ps[2][0:1, :], w3_sb[:, c:c + 1], h2_sb[:, c, :], start=(c == 0),
                               stop=(c == H2 // P - 1))
            mm.then_inc(top_done, 1)

        @block.scalar
        def _(act):
            act.wait_ge(small_in, 16)
            act.wait_ge(consts, 3)
            act.wait_ge(prep_pe, 1)
            for half in range(2):
                for ab in range(2):
                    last = act.copy(f_sb[D:D + 1, half, ab, :].rearrange("p (b q) -> p b q", q=PR),
                                    quad_ps[D:D + 1, 0:PR].unsqueeze(1).to_broadcast([1, QB, PR]))
            last.then_inc(prep_act, 1)
            act.wait_ge(prep_pe, 2)
            act.copy(ws_rows[:], turn_ps[:, 0:D].unsqueeze(1).to_broadcast([P, 2, D])).then_inc(prep_act, 1)
            act.activation(ws_grows[:], turn_ps[:, 0:D], ACT.Copy, scale=gs_sb[:, 0:1]).then_inc(prep_act, 1)
            act.wait_ge(prep_pe, 5)
            act.activation(x_sq[:], proj_ps[:, 0, 0, :], ACT.Square).then_inc(prep_act, 1)
            act.wait_ge(prep_pe, 6)
            act.activation(x_std[:], proj_ps[:, 0, 1, :], ACT.Sqrt, bias=eps[:, 0:1], scale=1.0 / EW).then_inc(prep_act, 1)
            act.wait_ge(prep_pe, 3)
            act.copy(gram[0:D, 0:D], mix_ps[0:D, 0:D])
            act.copy(gram[D:P, D:P], mix_ps[D:P, 0:D]).then_inc(prep_act, 1)
            act.wait_ge(prep_pe, 4)
            act.copy(proj_w[D:D + 1, :], ws_sb[D:D + 1, :])
            act.copy(proj_w[0:D, :], dots_ps[0:D, 0:EW]).then_inc(prep_act, 1)

            def square(chunk, q):
                s = chunk * QUARTERS + q
                act.wait_ge(projected, 2 * s + 2)
                wait(act, ssq_ready, s)
                act.activation(y_sq[:].rearrange("p b q -> p (b q)"),
                               proj_ps[:, q % 2, :, :].rearrange("p a n -> p (a n)"), ACT.Square).then_inc(sq_ready, 1)

            def save_cols(chunk, q):
                _, nt = tiles_of(q)
                s = chunk * QUARTERS + q
                act.wait_ge(turned, s + 1)
                wait(act, quad_done, s - 1)
                act.copy(e_cols[:, q % 2, 0:P * nt], turn_ps[:, 0:P * nt]).then_inc(cols_ready, 1)

            def save_f(chunk, q):
                s = chunk * QUARTERS + q
                act.wait_ge(mixed, s + 1)
                wait(act, projected, 2 * s - 2)
                for ab in range(2):
                    act.copy(f_sb[0:D, q % 2, ab, :], mix_ps[D * ab:D * (ab + 1), :]).then_inc(f_ready, 1)

            def root_n(chunk, q):
                s = chunk * QUARTERS + q
                act.wait_ge(var_ready, s + 1)
                act.activation(std_n[:], var_n[:], ACT.Sqrt, bias=eps[:, 0:1], scale=1.0 / EW).then_inc(std_ready, 1)

            def root_p(chunk, q):
                s = chunk * QUARTERS + q
                act.wait_ge(ssq_ready, s + 1)
                act.activation(std_p[:], var_p[:], ACT.Sqrt, bias=eps[:, 0:1], scale=1.0 / PR).then_inc(stdp_ready, 1)

            def place_x(chunk, q):
                s = chunk * QUARTERS + q
                act.wait_ge(prep_dve, 8)
                wait(act, dotted, s - 1)
                x = x_sb[:].rearrange("p (s k q a i) -> p s k q a i", s=CHUNKS, k=4, q=QUARTERS, a=2)
                for ab in range(2):
                    src = x[:, bass.ds(chunk, 1), :, q, ab, :].rearrange("p s k i -> p (s i) k")
                    last = act.copy(feats[:, q % 2, QB * ab:QB * (ab + 1), 0].rearrange("p (i k) -> p i k", k=4), src)
                last.then_inc(x_placed, 1)

            def save_z(chunk, q):
                s = chunk * QUARTERS + q
                act.wait_ge(dotted, s + 1)
                n = 2 * QB // 4
                act.copy(z_mine[:, bass.ds(chunk, 1), :, n * q:n * (q + 1)].rearrange("p s c g -> p (s c) g"),
                         dots_ps[:, 0:PR * n].rearrange("p (g c) -> p c g", c=PR)).then_inc(z_saved, 1)

            slots(act, [(2, square), (0, save_cols), (1, save_f), (2, root_p), (0, root_n), (2, place_x), (3, save_z)])

            act.wait_ge(prep_pe, 7)
            act.wait_ge(top_in, 32)
            for j in range(MAXD // P):
                act.wait_ge(o_done, j + 1)
                act.activation(o_sq[:, j, :], proj_ps[:, j // 2, j % 2, :], ACT.Square).then_inc(osq_done, 1)
            act.wait_ge(ovar_done, 1)
            act.activation(o_std[:], mix_ps[:], ACT.Sqrt, bias=eps[:, 0:1], scale=1.0 / MAXD).then_inc(ostd_done, 1)
            act.wait_ge(prep_dve, 10)
            h1_ps = [turn_ps[:], quad_ps[:], dots_ps[:], mix_ps[:]]
            for j in range(H1 // P):
                act.wait_ge(h1_done, j + 1)
                act.activation(h1_sb[:, j, :], h1_ps[j], ACT.Relu, bias=b1_all[:, j:j + 1]).then_inc(h1_ready, 1)
            for j in range(H2 // P):
                act.wait_ge(h2_done, j + 1)
                act.activation(h2_sb[:, j, :], proj_ps[:, 0, j, :], ACT.Relu, bias=b2_sb[:, j:j + 1]).then_inc(h2_ready, 1)
            act.wait_ge(top_done, 1)
            act.copy(y_out[:], proj_ps[0:1, 1, 0, :]).then_inc(y_done, 1)

        @block.vector
        def _(dve):
            links = [0]

            def link(instruction):
                links[0] += 1
                instruction.then_inc(chain, 1)
                dve.wait_ge(chain, links[0])

            def centre(out, in_, mean, width):
                link(dve.tensor_reduce(mean, in_, AX.X, ALU.add))
                link(dve.tensor_scalar(mean, mean, 1.0 / width, None, ALU.mult))
                return dve.tensor_tensor(out, in_, mean.unsqueeze(2).to_broadcast(list(in_.shape)), ALU.subtract)

            dve.wait_ge(ids_in, 32)
            dve.tensor_tensor(rows_sb[:], ids_sb[:], offs_sb[:], ALU.add).then_inc(rows_ready, 1)
            dve.wait_ge(small_in, 16)
            centre(ws_c[:].unsqueeze(1), ws_sb[0:D, :].unsqueeze(1), ws_mean[:], EW).then_inc(prep_dve, 1)
            centre(wsi_c[:].unsqueeze(1), wsi_sb[0:NF, :].unsqueeze(1), wsi_mean[:], PR).then_inc(prep_dve, 1)
            dve.wait_ge(dense_in, 32)
            centre(wd_c[:], wd_sb[:], wd_mean[:], EW).then_inc(prep_dve, 1)
            dve.wait_ge(mixw_in, 16)
            centre(mixw_c[:], mixw_sb[:], mixw_mean[:], PR).then_inc(prep_dve, 1)
            dve.wait_ge(prep_act, 5)
            dve.reciprocal(x_rstd[:], x_std[:]).then_inc(prep_dve, 1)
            dve.wait_ge(prep_dve, 5)
            dve.tensor_tensor(x_unit[:], proj_ps[:, 0, 0, :], x_rstd[:], ALU.mult).then_inc(prep_dve, 1)
            dve.wait_ge(prep_dve, 6)
            dve.tensor_scalar(x_sb[:], x_unit[:], gd_sb[:, 0:1], bd_sb[:, 0:1], ALU.mult, ALU.add).then_inc(prep_dve, 1)
            dve.memset(var_n[:], 1.0).then_inc(prep_dve, 1)
            dve.wait_ge(prep_dve, 8)

            def variance_p(chunk, q):
                s = chunk * QUARTERS + q
                dve.wait_ge(sq_ready, s + 1)
                wait(dve, stdp_ready, s)
                dve.tensor_reduce(var_p[:], y_sq[:], AX.X, ALU.add).then_inc(ssq_ready, 1)

            def variance_n(chunk, q):
                t0, nt = tiles_of(q)
                s = chunk * QUARTERS + q
                dve.wait_ge(quad_done, s + 1)
                wait(dve, std_ready, s)
                dve.wait_ge(gathered[q], chunk * (32 * nt) + 32 * nt)
                dve.tensor_tensor(e_prod[:, 0:2 * nt, :].rearrange("p a d -> p (a d)"), quad_ps[:, 0:P * nt],
                                  e_rows[:, t0:t0 + nt, :].rearrange("p t d -> p (t d)"), ALU.mult).then_inc(prod_done, 1)
                dve.wait_ge(prod_done, s + 1)
                dve.tensor_reduce(var_n[:, 0:2 * nt], e_prod[:, 0:2 * nt, :], AX.X, ALU.add).then_inc(var_ready, 1)

            def norm_p(chunk, q):
                s = chunk * QUARTERS + q
                wide = [P, 2 * QB, PR]
                dve.wait_ge(stdp_ready, s + 1)
                dve.reciprocal(rstd_p[:], std_p[:]).then_inc(rstdp_done, 1)
                dve.wait_ge(rstdp_done, s + 1)
                dve.tensor_tensor(y_a[:], proj_ps[:, q % 2, :, :].rearrange("p a (b q) -> p (a b) q", q=PR),
                                  rstd_p[:].unsqueeze(2).to_broadcast(wide), ALU.mult).then_inc(y_unit, 1)
                dve.wait_ge(y_unit, s + 1)
                dve.tensor_tensor(y_b[:], y_a[:], gsi_sb.unsqueeze(1).to_broadcast(wide), ALU.mult).then_inc(y_gained, 1)
                dve.wait_ge(y_gained, s + 1)
                wait(dve, dotted, s - 1)
                dve.tensor_tensor(feats[:, q % 2, :, 1:PR + 1], y_b[:], bsi_sb.unsqueeze(1).to_broadcast(wide),
                                  ALU.add).then_inc(y_ready, 1)

            def norm_n(chunk, q):
                t0, nt = tiles_of(q)
                s = chunk * QUARTERS + q
                dve.wait_ge(std_ready, s + 1)
                dve.reciprocal(rstd_n[:], std_n[:]).then_inc(rstdn_done, 1)
                dve.wait_ge(rstdn_done, s + 1)
                wait(dve, mixed, s - QUARTERS + 1 + (q < QUARTERS - 1))
                dve.tensor_tensor(e_unit[:, t0:t0 + nt, :].rearrange("p t (a d) -> p (t a) d", d=D),
                                  e_rows[:, t0:t0 + nt, :].rearrange("p t (a d) -> p (t a) d", d=D),
                                  rstd_n[:, 0:2 * nt].unsqueeze(2).to_broadcast([P, 2 * nt, D]),
                                  ALU.mult).then_inc(unit_ready, 1)

            def top_weights():
                dve.wait_ge(wl_in, 16)
                centre(wl_c[:], wl_sb[:], wl_mean[:], MAXD)
                dve.wait_ge(top_in, 32)
                for c in range(KU):
                    last = dve.tensor_scalar(w1_g[:, c, :], w1_sb[:, c, :], gl_sb[:, c:c + 1], None, ALU.mult)
                last.then_inc(prep_dve, 1)

            slots(dve, [(2, variance_p), (0, variance_n), (2, norm_p), (0, norm_n)], once=top_weights)

            dve.wait_ge(prep_pe, 7)
            dve.tensor_tensor(b1_all[:], dots_ps[:, 0:H1 // P], b1_sb, ALU.add).then_inc(prep_dve, 1)
            dve.wait_ge(ostd_done, 1)
            link(dve.reciprocal(o_rstd[:], o_std[:]))
            for c in range(KU):
                dve.wait_ge(o_done, c + 1)
                dve.tensor_tensor(z_unit[:, c, :], proj_ps[:, c // 2, c % 2, :], o_rstd[:], ALU.mult).then_inc(zu_done, 1)


def kernel(**inputs):
    import concourse.bacc as bacc
    from concourse.bass_utils import run_bass_kernel_spmd

    a = {k: np.asarray(v) for k, v in inputs.items()}

    def by_partition(m):
        return np.ascontiguousarray(m.reshape(-1, P, m.shape[1]).transpose(1, 0, 2))

    def columns(v):
        return np.ascontiguousarray(v.reshape(-1, P).T)

    order = np.arange(B).reshape(CHUNKS, 2, QUARTERS, QB // 4, 4).transpose(0, 4, 2, 1, 3).reshape(-1)
    small = np.zeros((P, PACKED), np.float32)

    def put(name, v):
        begin, end = PACK[name]
        small[:v.shape[0], begin:end] = v

    put("eye", np.eye(P, dtype=np.float32))
    put("ws", np.concatenate([a["L0_rec_Ws"].T, a["L0_rec_bs"][None]]))
    put("wsi", a["L0_rec_Wsi"].T)
    put("gsi", np.broadcast_to(a["L0_rec_gsi"], (P, PR)))
    put("bsi", np.broadcast_to(a["L0_rec_bsi"], (P, PR)))
    put("gs", columns(a["L0_rec_gs"]))
    put("gd", columns(a["L0_rec_gd"]))
    put("bd", columns(a["L0_rec_bd"]))
    put("gl", columns(a["L0_rec_gl"][:USED]))
    put("bl", columns(a["L0_rec_bl"][:USED]))
    put("b1", columns(a["b_top1"]))
    put("b2", columns(a["b_top2"]))
    put("w3", columns(a["W_top3"][:, 0]))

    row = np.arange(TILES * P).reshape(TILES, P)
    sample, feature = row // NF, row % NF
    starts = np.concatenate([[0], np.cumsum(VOCAB)[:-1]]).astype(np.int32)
    offs = np.broadcast_to(starts[feature].T[:, None, :, None], (P, CHUNKS, TILES, 2)).reshape(P, -1)
    ids = a["ids"].reshape(CHUNKS, 2, TILES, P).transpose(3, 0, 2, 1).reshape(P, -1)
    mixw = np.zeros((P, TILES, SPAN, PR), np.float32)
    for t in range(TILES):
        mixw[np.arange(P), t, sample[t] - first_sample(t)] = a["L0_rec_Wsi"].T[feature[t]]
    wl = np.zeros((4, PR, KZ, MAXD), np.float32)
    for c in range(PR):
        for p in range(c, PR):
            wl[c // KZ, p, c % KZ] = a["L0_rec_Wl"][:, (p + 1) * p // 2 + c]
    w1 = a["W_top1"]
    arrays = {
        "table": np.concatenate([a[f"tbl_{n}"] for n in range(NF)]),
        "ids": np.ascontiguousarray(ids),
        "offs": np.ascontiguousarray(offs),
        "small": small,
        "mixw": mixw.reshape(P, TILES * SPAN, PR),
        "dense_t": by_partition(np.ascontiguousarray(a["r_dense_t"][order].T)),
        "wd_t": by_partition(np.ascontiguousarray(a["L0_rec_Wd"].T)),
        "wl": wl.reshape(P, KZ, MAXD),
        "w1": by_partition(np.concatenate([w1[:USED], w1[MAXD:]])),
        "w2": by_partition(a["W_top2"]),
    }
    nc = bacc.Bacc("TRN2", target_bir_lowering=False, num_devices=1)
    args = [nc.dram_tensor(f"{name}_dram", v.shape, mybir.dt.from_np(v.dtype), kind="ExternalInput").ap()
            for name, v in arrays.items()]
    args.append(nc.dram_tensor("out_dram", (1, B), F32, kind="ExternalOutput").ap())
    tower(nc, *args)
    r = run_bass_kernel_spmd(nc, [{f"{name}_dram": v for name, v in arrays.items()}], core_ids=[0])
    y = np.empty((B, 1), np.float32)
    y[order, 0] = r.results[0]["out_dram"][0]
    return y
```

```python
from contextlib import ExitStack

import numpy as np

import concourse.bass as bass
from concourse import mybir

ALU = mybir.AluOpType
ACT = mybir.ActivationFunctionType
AX = mybir.AxisListType
F32 = mybir.dt.float32
I32 = mybir.dt.int32

P = 128
VOCAB = [1000, 125000, 1000, 12500, 12500, 12500, 1000, 12500, 1000, 1250, 125000, 1250, 1250, 1000,
         1000, 1250, 1000, 1250, 125000, 1000, 1250, 1000, 12500, 1000, 1000, 1000]
NF = len(VOCAB)
D = 64
EW = 128
PR = 32
B = 512
CHUNKS = B // P
HALF = P // 2
TILES = HALF * NF // P
QUARTERS = 4
QB = HALF // QUARTERS
SLOTS = CHUNKS * QUARTERS
SPAN = 6
MAXD = 512
USED = 384
DENSE = 256
H1 = 512
H2 = 256
KZ = PR * PR // P
KU = USED // P
KD = DENSE // P
EPS = 1e-5


def first_sample(t):
    return P * t // NF


def tiles_of(q):
    end = [-(-(q1 + 1) * QB * NF // P) for q1 in range(QUARTERS)]
    begin = end[q - 1] if q else 0
    return begin, end[q] - begin


def mix_parts(q):
    parts = []
    for t in range(TILES):
        lo = max(q * QB, first_sample(t))
        hi = min((q + 1) * QB, (P * (t + 1) - 1) // NF + 1)
        if lo < hi:
            parts.append((t, lo - first_sample(t), lo - q * QB, hi - lo))
    return parts


PACK = {}
for _name, _width in (("eye", P), ("ws", EW), ("wsi", PR), ("gsi", PR), ("bsi", PR), ("gs", 1), ("gd", 1), ("bd", 1),
                      ("gl", USED // P), ("bl", USED // P), ("b1", H1 // P), ("b2", H2 // P), ("w3", H2 // P)):
    _at = max([end for _, end in PACK.values()], default=0)
    PACK[_name] = (_at, _at + _width)
PACKED = max(end for _, end in PACK.values())


def tower(nc, table, ids, offs, small, row_w, owner, dense_t, wd_t, wl, w1, w2, out):
    with ExitStack() as ctx:
        def sb(name, shape, dt=F32):
            return ctx.enter_context(nc.sbuf_tensor(name, shape, dt))

        def psum(name, shape):
            return ctx.enter_context(nc.psum_tensor(name, shape, F32))

        def sem(name):
            return ctx.enter_context(nc.semaphore(name))

        turn_ps = psum("turn_ps", [P, 512])
        quad_ps = psum("quad_ps", [P, 512])
        mix_ps = psum("mix_ps", [P, 512])
        dots_ps = psum("dots_ps", [P, 512])
        proj_ps = psum("proj_ps", [P, 2, 2, 512])

        o_ps = [turn_ps[:], quad_ps[:], mix_ps[:], proj_ps[:, 0, 0, :]]
        bl_ps = dots_ps
        dense_ps = [proj_ps[:, 1, 0, :], proj_ps[:, 1, 1, :], dots_ps[:], dots_ps[:]]
        ovar_ps = proj_ps[:, 1, 0, :]
        h1_ps = [dots_ps[:], proj_ps[:, 0, 1, :], proj_ps[:, 1, 1, :], o_ps[0]]
        h2_ps = o_ps[1:3]
        y_ps = o_ps[3][0:1, :]

        ids_sb = sb("ids_sb", [P, CHUNKS * TILES * 2], I32)
        offs_sb = sb("offs_sb", [P, CHUNKS * TILES * 2], I32)
        rows_sb = sb("rows_sb", [P, CHUNKS * TILES * 2], I32)
        e_rows = sb("e_rows", [P, TILES, 2 * D])
        e_unit = sb("e_unit", [P, TILES, 2 * D])
        e_cols = sb("e_cols", [P, 2, 4 * P])
        e_prod = sb("e_prod", [P, 4 * 2, D])
        var_n = sb("var_n", [P, 8])
        std_n = sb("std_n", [P, 8])
        rstd_n = sb("rstd_n", [P, 8])
        f_sb = sb("f_sb", [D + 1, 2, 2, 512])
        y_sq = sb("y_sq", [P, 2 * QB, PR])
        var_p = sb("var_p", [P, 2 * QB])
        std_p = sb("std_p", [P, 2 * QB])
        rstd_p = sb("rstd_p", [P, 2 * QB])
        y_a = sb("y_a", [P, 2 * QB, PR])
        y_b = sb("y_b", [P, 2 * QB, PR])
        feats = sb("feats", [P, 2, 2 * QB, PR + 1])
        z_mine = sb("z_mine", [P, CHUNKS, PR, PR])
        z_pairs = sb("z_pairs", [P, CHUNKS, 4, KZ, PR])

        small_sb = sb("small_sb", [P, PACKED])
        eye_sb, ws_sb, wsi_sb, gsi_sb, bsi_sb, gs_sb, gd_sb, bd_sb, gl_sb, bl_sb, b1_sb, b2_sb, w3_sb = (
            small_sb[:, begin:end] for begin, end in PACK.values())
        ones = sb("ones", [P, P])
        eps = sb("eps", [P, 1])
        mixw_sb = sb("mixw_sb", [P, TILES, SPAN, PR])
        row_w_sb = sb("row_w_sb", [P, TILES, PR])
        row_w_mean = sb("row_w_mean", [P, TILES])
        owner_sb = sb("owner_sb", [P, TILES, SPAN])
        wsi_mean = sb("wsi_mean", [NF, 1])
        wsi_c = sb("wsi_c", [NF, PR])
        ws_mean = sb("ws_mean", [D, 1])
        ws_c = sb("ws_c", [D, EW])
        ws_rows = sb("ws_rows", [EW, 2, D])
        ws_grows = sb("ws_grows", [EW, D])
        gram = sb("gram", [P, P])
        proj_w = sb("proj_w", [D + 1, EW])
        dense_sb = sb("dense_sb", [P, KD, B])
        wd_sb = sb("wd_sb", [P, KD, EW])
        wd_mean = sb("wd_mean", [P, KD])
        wd_c = sb("wd_c", [P, KD, EW])
        x_sq = sb("x_sq", [P, B])
        x_std = sb("x_std", [P, B])
        x_rstd = sb("x_rstd", [P, B])
        x_unit = sb("x_unit", [P, B])
        x_sb = sb("x_sb", [P, B])
        wl_sb = sb("wl_sb", [P, KZ, MAXD])
        wl_mean = sb("wl_mean", [P, KZ])
        w1_sb = sb("w1_sb", [P, KU + KD, H1])
        w1_g = sb("w1_g", [P, KU, H1])
        b1_all = sb("b1_all", [P, H1 // P])
        w2_sb = sb("w2_sb", [P, H1 // P, H2])
        o_sq = sb("o_sq", [P, MAXD // P, B])
        o_std = sb("o_std", [P, B])
        o_rstd = sb("o_rstd", [P, B])
        h1_sum = o_sq
        o_sb = sb("o_sb", [P, KU, B])
        h1_dense = sb("h1_dense", [P, H1 // P, B])
        h1_sb = sb("h1_sb", [P, H1 // P, B])
        h2_sb = sb("h2_sb", [P, H2 // P, B])
        h1_unit = h1_sb
        y_out = sb("y_out", [1, B])

        ids_in, small_in, mixw_in, dense_in = sem("ids_in"), sem("small_in"), sem("mixw_in"), sem("dense_in")
        w1_in, wl_in, w2_in, out_done = sem("w1_in"), sem("wl_in"), sem("w2_in"), sem("out_done")
        gathered = [sem(f"gathered{q}") for q in range(QUARTERS)]
        rows_ready = sem("rows_ready")
        consts = sem("consts")
        prep_dve, prep_pe, prep_act = sem("prep_dve"), sem("prep_pe"), sem("prep_act")
        turned, cols_ready, quad_done, var_ready, std_ready, unit_ready = (
            sem(n) for n in ("turned", "cols_ready", "quad_done", "var_ready", "std_ready", "unit_ready"))
        mixed, f_ready, projected, sq_ready, ssq_ready, stdp_ready = (
            sem(n) for n in ("mixed", "f_ready", "projected", "sq_ready", "ssq_ready", "stdp_ready"))
        y_ready, x_placed, dotted, z_saved, z_moved = (
            sem(n) for n in ("y_ready", "x_placed", "dotted", "z_saved", "z_moved"))
        chain = sem("chain")
        prod_done, rstdn_done, rstdp_done, y_unit, y_gained = (
            sem(n) for n in ("prod_done", "rstdn_done", "rstdp_done", "y_unit", "y_gained"))
        o_done, osq_done, ovar_done, ostd_done, o_saved, z_by_act, z_by_dve, x_ready = (
            sem(n) for n in ("o_done", "osq_done", "ovar_done", "ostd_done", "o_saved", "z_by_act", "z_by_dve",
                             "x_ready"))
        bl_done, b1_ready, dense_done, dense_saved, wl_mean_ready, wl_ready, w1_ready, h1_summed = (
            sem(n) for n in ("bl_done", "b1_ready", "dense_done", "dense_saved", "wl_mean_ready", "wl_ready",
                             "w1_ready", "h1_summed"))
        h1_done, h1_ready, h2_done, h2_ready, top_done, y_done = (
            sem(n) for n in ("h1_done", "h1_ready", "h2_done", "h2_ready", "top_done", "y_done"))

        block = ctx.enter_context(nc.Block())

        def slots(eng, stages, extra=()):
            latest = max(late for late, _ in stages)
            extra = dict(extra)

            def slot(chunk, q, s=None):
                for late, stage in stages:
                    if s is None or 0 <= s - late < SLOTS:
                        stage(chunk + (q - late) // QUARTERS, (q - late) % QUARTERS)
                if s in extra:
                    extra[s]()

            peeled = -(-latest // QUARTERS) * QUARTERS
            for s in range(peeled):
                slot(s // QUARTERS, s % QUARTERS, s)
            with eng.Fori(peeled // QUARTERS, CHUNKS) as chunk:
                for q in range(QUARTERS):
                    slot(chunk, q)
            for s in range(SLOTS, SLOTS + latest):
                slot(s // QUARTERS, s % QUARTERS, s)

        def wait(eng, semaphore, count):
            if not isinstance(count, int) or count > 0:
                eng.wait_ge(semaphore, count)

        def move_last(copy, blocks):
            for k, c in blocks:
                last = copy(z_pairs[PR * c:PR * (c + 1), CHUNKS - 1, k, :, :],
                            z_mine[PR * k:PR * (k + 1), CHUNKS - 1, KZ * c:KZ * (c + 1), :])
            return last

        blocks = [(k, c) for k in range(4) for c in range(4)]

        @block.sync
        def _(sp):
            sp.dma_start(ids_sb[:], ids).then_inc(ids_in, 16)
            sp.dma_start(offs_sb[:], offs).then_inc(ids_in, 16)
            sp.dma_start(small_sb[:], small).then_inc(small_in, 16)
            sp.dma_start(wd_sb[:], wd_t).then_inc(dense_in, 16)
            sp.dma_start(dense_sb[:], dense_t).then_inc(dense_in, 16)
            sp.dma_start(row_w_sb[:], row_w).then_inc(mixw_in, 16)
            sp.dma_start(owner_sb[:], owner).then_inc(mixw_in, 16)
            sp.dma_start(w1_sb[:], w1).then_inc(w1_in, 16)
            sp.dma_start(wl_sb[:], wl).then_inc(wl_in, 16)
            sp.dma_start(w2_sb[:], w2).then_inc(w2_in, 16)
            with sp.Fori(0, CHUNKS - 1) as chunk:
                sp.wait_ge(z_saved, chunk * QUARTERS + QUARTERS)
                for k in range(4):
                    for c in range(4):
                        sp.dma_start(
                            z_pairs[PR * c:PR * (c + 1), bass.ds(chunk, 1), k, :, :],
                            z_mine[PR * k:PR * (k + 1), bass.ds(chunk, 1), KZ * c:KZ * (c + 1), :],
                        ).then_inc(z_moved, 16)
            sp.wait_ge(y_done, 1)
            sp.dma_start(out, y_out[:]).then_inc(out_done, 16)
            sp.wait_ge(out_done, 16)

        @block.gpsimd
        def _(pool):
            pool.memset(ones[:], 1.0).then_inc(consts, 1)
            pool.memset(eps[:], EPS).then_inc(consts, 1)
            pool.memset(gram[:], 0.0).then_inc(consts, 1)
            pool.wait_ge(rows_ready, 1)
            for chunk in range(CHUNKS):
                for q in range(QUARTERS):
                    wait(pool, unit_ready, QUARTERS * (chunk - 1) + q + 1)
                    t0, nt = tiles_of(q)
                    for t in range(t0, t0 + nt):
                        for ab in range(2):
                            col = (chunk * TILES + t) * 2 + ab
                            pool.indirect_dma_start(
                                out=e_rows[:, t, D * ab:D * (ab + 1)], out_offset=None, in_=table,
                                in_offset=bass.IndirectOffsetOnAxis(ap=rows_sb[:, col:col + 1], axis=0),
                            ).then_inc(gathered[q], 16)

        @block.tensor
        def _(pe):
            pe.wait_ge(small_in, 16)
            pe.wait_ge(consts, 3)
            pe.wait_ge(prep_dve, 2)
            pe.matmul(quad_ps[:, 0:PR], ones[0:NF, :], wsi_c[:], start=True, stop=True).then_inc(prep_pe, 1)
            pe.transpose(turn_ps[:, 0:D], ws_c[:], eye_sb[0:D, 0:D]).then_inc(prep_pe, 1)
            pe.wait_ge(prep_act, 2)
            pe.matmul(mix_ps[:, 0:D], ws_rows[:].rearrange("p a d -> p (a d)"), ws_rows[:, 0, :], start=True,
                      stop=True).then_inc(prep_pe, 1)
            pe.wait_ge(prep_act, 3)
            pe.transpose(dots_ps[0:D, 0:EW], ws_grows[:], eye_sb).then_inc(prep_pe, 1)
            pe.wait_ge(dense_in, 32)
            pe.wait_ge(prep_dve, 3)
            for j in range(KD):
                mm = pe.matmul(proj_ps[:, 0, 0, :], wd_c[:, j, :], dense_sb[:, j, :], start=(j == 0), stop=(j == KD - 1))
            mm.then_inc(prep_pe, 1)
            pe.wait_ge(prep_act, 6)
            pe.matmul(proj_ps[:, 0, 1, :], ones[:], x_sq[:], start=True, stop=True).then_inc(prep_pe, 1)
            def top_dense(j):
                for c in range(KD):
                    mm = pe.matmul(dense_ps[j], w1_sb[:, KU + c, P * j:P * (j + 1)], dense_sb[:, c, :],
                                   start=(c == 0), stop=(c == KD - 1))
                mm.then_inc(dense_done, 1)

            def top_early():
                pe.wait_ge(w1_in, 16)
                for j in range(H1 // P):
                    for c in range(KU):
                        mm = pe.matmul(bl_ps[:, j:j + 1], w1_sb[:, c, P * j:P * (j + 1)], bl_sb[:, c:c + 1],
                                       start=(c == 0), stop=(c == KU - 1))
                mm.then_inc(bl_done, 1)
                top_dense(0)
                top_dense(1)
                pe.wait_ge(x_ready, 1)

            def top_middle():
                pe.wait_ge(b1_ready, 1)
                top_dense(2)
                pe.wait_ge(dense_saved, 2)

            def top_late():
                pe.wait_ge(dense_saved, 3)
                top_dense(3)
                pe.wait_ge(dense_saved, 4)

            def turn(chunk, q):
                t0, nt = tiles_of(q)
                s = chunk * QUARTERS + q
                pe.wait_ge(gathered[q], chunk * (32 * nt) + 32 * nt)
                wait(pe, cols_ready, s)
                for t in range(nt):
                    mm = pe.transpose(turn_ps[:, P * t:P * (t + 1)], e_rows[:, t0 + t, :], eye_sb)
                mm.then_inc(turned, 1)

            def mix(chunk, q):
                s = chunk * QUARTERS + q
                pe.wait_ge(unit_ready, s + 1)
                wait(pe, f_ready, 2 * s)
                for n, (t, lo, at, number) in enumerate(mix_parts(q)):
                    mm = pe.matmul(mix_ps[:, PR * at:PR * (at + number)], e_unit[:, t, :],
                                   mixw_sb[:, t, lo:lo + number, :].rearrange("k b p -> k (b p)"),
                                   start=(n == 0), stop=(n == len(mix_parts(q)) - 1), skip_group_check=True)
                mm.then_inc(mixed, 1)

            def quad(chunk, q):
                _, nt = tiles_of(q)
                s = chunk * QUARTERS + q
                pe.wait_ge(cols_ready, s + 1)
                wait(pe, var_ready, s)
                for t in range(nt):
                    mm = pe.matmul(quad_ps[:, P * t:P * (t + 1)], e_cols[:, q % 2, P * t:P * (t + 1)], gram[:],
                                   start=True, stop=True)
                mm.then_inc(quad_done, 1)

            def dots(chunk, q):
                s = chunk * QUARTERS + q
                pe.wait_ge(y_ready, s + 1)
                pe.wait_ge(x_placed, s + 1)
                wait(pe, z_saved, s)
                for g in range(2 * QB // 4):
                    for k in range(4):
                        f = feats[:, q % 2, 4 * g + k, :]
                        mm = pe.matmul(dots_ps[PR * k:PR * (k + 1), PR * g:PR * (g + 1)], f[:, 1:PR + 1], f[:, 0:PR],
                                       start=True, stop=True)
                mm.then_inc(dotted, 1)

            def project(chunk, q):
                s = chunk * QUARTERS + q
                wait(pe, y_ready, s - 1)
                for ab in range(2):
                    pe.wait_ge(f_ready, 2 * s + ab + 1)
                    pe.matmul(proj_ps[:, q % 2, ab, :], proj_w[:], f_sb[:, q % 2, ab, :], start=True,
                              stop=True).then_inc(projected, 1)

            def chunks_o(j, first, number):
                for c in range(KZ):
                    mm = pe.matmul(o_ps[j][:, P * first:P * (first + number)], wl_sb[:, c, P * j:P * (j + 1)],
                                   z_pairs[:, first:first + number, :, c, :].rearrange("p s k g -> p (s k) g"),
                                   start=(c == 0), stop=(c == KZ - 1))
                return mm

            def early_o(j):
                if j == 0:
                    pe.wait_ge(wl_ready, 1)
                    pe.wait_ge(z_moved, 16 * 16 * (CHUNKS - 1))
                    pe.wait_ge(cols_ready, SLOTS)
                if j == 1:
                    pe.wait_ge(var_ready, SLOTS)
                if j == 2:
                    pe.wait_ge(f_ready, 2 * SLOTS)
                chunks_o(j, 0, CHUNKS - 1)

            slots(pe, [(1, quad), (2, mix), (0, turn), (4, dots), (2, project)],
                  extra=[(1, top_early), (2, top_middle), (3, top_late)] + [(SLOTS + 1, lambda: early_o(0)), (SLOTS + 2, lambda: early_o(1)),
                                                                      (SLOTS + 3, lambda: early_o(2))])

            pe.wait_ge(y_unit, SLOTS)
            chunks_o(3, 0, CHUNKS - 1)
            pe.wait_ge(z_by_act, 1)
            pe.wait_ge(z_by_dve, 1)
            for j in range(MAXD // P):
                chunks_o(j, CHUNKS - 1, 1).then_inc(o_done, 1)

            def add_squares(j):
                pe.wait_ge(osq_done, j + 1)
                return pe.matmul(ovar_ps, ones[:], o_sq[:, j, :], start=(j == 0), stop=(j == MAXD // P - 1))

            for j in range(MAXD // P - 1):
                add_squares(j)
            pe.wait_ge(z_saved, SLOTS)
            pe.wait_ge(w1_ready, 1)
            pe.wait_ge(w2_in, 16)
            for j in range(H1 // P):
                for c in range(KU):
                    pe.wait_ge(o_saved, c + 1)
                    mm = pe.matmul(h1_ps[j], w1_g[:, c, P * j:P * (j + 1)], o_sb[:, c, :], start=(c == 0),
                                   stop=(c == KU - 1))
                mm.then_inc(h1_done, 1)
                if j == 0:
                    add_squares(MAXD // P - 1).then_inc(ovar_done, 1)
            for c in range(H1 // P):
                pe.wait_ge(h1_ready, c + 1)
                for j in range(H2 // P):
                    mm = pe.matmul(h2_ps[j], w2_sb[:, c, P * j:P * (j + 1)], h1_sb[:, c, :], start=(c == 0),
                                   stop=(c == H1 // P - 1), skip_group_check=True)
                    if c == H1 // P - 1:
                        mm.then_inc(h2_done, 1)
            for c in range(H2 // P):
                pe.wait_ge(h2_ready, c + 1)
                mm = pe.matmul(y_ps, w3_sb[:, c:c + 1], h2_sb[:, c, :], start=(c == 0), stop=(c == H2 // P - 1))
            mm.then_inc(top_done, 1)

        @block.scalar
        def _(act):
            act.wait_ge(consts, 3)
            act.activation(x_std[:, 0:1], eps[:, 0:1], ACT.Sqrt)
            act.wait_ge(small_in, 16)
            act.wait_ge(prep_pe, 1)
            for half in range(2):
                for ab in range(2):
                    last = act.copy(f_sb[D:D + 1, half, ab, :].rearrange("p (b q) -> p b q", q=PR),
                                    quad_ps[D:D + 1, 0:PR].unsqueeze(1).to_broadcast([1, QB, PR]))
            last.then_inc(prep_act, 1)
            act.wait_ge(prep_pe, 2)
            act.copy(ws_rows[:], turn_ps[:, 0:D].unsqueeze(1).to_broadcast([P, 2, D])).then_inc(prep_act, 1)
            act.activation(ws_grows[:], turn_ps[:, 0:D], ACT.Copy, scale=gs_sb[:, 0:1]).then_inc(prep_act, 1)
            act.wait_ge(prep_pe, 3)
            act.copy(gram[0:D, 0:D], mix_ps[0:D, 0:D])
            act.copy(gram[D:P, D:P], mix_ps[D:P, 0:D]).then_inc(prep_act, 1)
            act.wait_ge(prep_pe, 4)
            act.copy(proj_w[D:D + 1, :], ws_sb[D:D + 1, :])
            act.copy(proj_w[0:D, :], dots_ps[0:D, 0:EW]).then_inc(prep_act, 1)
            act.wait_ge(prep_pe, 5)
            act.activation(x_sq[:], proj_ps[:, 0, 0, :], ACT.Square).then_inc(prep_act, 1)
            act.wait_ge(prep_pe, 6)
            act.activation(x_std[:], proj_ps[:, 0, 1, :], ACT.Sqrt, bias=eps[:, 0:1], scale=1.0 / EW).then_inc(prep_act, 1)

            def square(chunk, q):
                s = chunk * QUARTERS + q
                act.wait_ge(projected, 2 * s + 2)
                wait(act, ssq_ready, s)
                act.activation(y_sq[:].rearrange("p b q -> p (b q)"),
                               proj_ps[:, q % 2, :, :].rearrange("p a n -> p (a n)"), ACT.Square).then_inc(sq_ready, 1)

            def save_cols(chunk, q):
                _, nt = tiles_of(q)
                s = chunk * QUARTERS + q
                act.wait_ge(turned, s + 1)
                wait(act, quad_done, s - 1)
                act.copy(e_cols[:, q % 2, 0:P * nt], turn_ps[:, 0:P * nt]).then_inc(cols_ready, 1)

            def save_f(chunk, q):
                s = chunk * QUARTERS + q
                act.wait_ge(mixed, s + 1)
                wait(act, projected, 2 * s - 2)
                for ab in range(2):
                    act.copy(f_sb[0:D, q % 2, ab, :], mix_ps[D * ab:D * (ab + 1), :]).then_inc(f_ready, 1)

            def root_n(chunk, q):
                s = chunk * QUARTERS + q
                act.wait_ge(var_ready, s + 1)
                act.activation(std_n[:], var_n[:], ACT.Sqrt, bias=eps[:, 0:1], scale=1.0 / EW).then_inc(std_ready, 1)

            def root_p(chunk, q):
                s = chunk * QUARTERS + q
                act.wait_ge(ssq_ready, s + 1)
                act.activation(std_p[:], var_p[:], ACT.Sqrt, bias=eps[:, 0:1], scale=1.0 / PR).then_inc(stdp_ready, 1)

            def place_x(chunk, q):
                s = chunk * QUARTERS + q
                act.wait_ge(x_ready, 1)
                wait(act, dotted, s - 1)
                x = x_sb[:].rearrange("p (s k q a i) -> p s k q a i", s=CHUNKS, k=4, q=QUARTERS, a=2)
                for ab in range(2):
                    src = x[:, bass.ds(chunk, 1), :, q, ab, :].rearrange("p s k i -> p (s i) k")
                    last = act.copy(feats[:, q % 2, QB * ab:QB * (ab + 1), 0].rearrange("p (i k) -> p i k", k=4), src)
                last.then_inc(x_placed, 1)

            def save_z(chunk, q):
                s = chunk * QUARTERS + q
                act.wait_ge(dotted, s + 1)
                n = 2 * QB // 4
                act.copy(z_mine[:, bass.ds(chunk, 1), :, n * q:n * (q + 1)].rearrange("p s c g -> p (s c) g"),
                         dots_ps[:, 0:PR * n].rearrange("p (g c) -> p c g", c=PR)).then_inc(z_saved, 1)

            def save_dense(first, number):
                act.wait_ge(b1_ready, 1)
                for j in range(first, first + number):
                    act.wait_ge(dense_done, j + 1)
                    act.activation(h1_dense[:, j, :], dense_ps[j], ACT.Identity,
                                   bias=b1_all[:, j:j + 1]).then_inc(dense_saved, 1)

            def centre_wl():
                act.wait_ge(wl_mean_ready, 1)
                for c in range(KZ):
                    last = act.activation(wl_sb[:, c, :], wl_sb[:, c, :], ACT.Identity, bias=wl_mean[:, c:c + 1])
                last.then_inc(wl_ready, 1)

            def gain_w1():
                for c in range(KU):
                    last = act.activation(w1_g[:, c, :], w1_sb[:, c, :], ACT.Copy, scale=gl_sb[:, c:c + 1])
                last.then_inc(w1_ready, 1)

            slots(act, [(3, square), (3, root_p), (2, save_f), (1, root_n), (0, save_cols), (3, place_x), (4, save_z)],
                  extra=[(2, lambda: save_dense(0, 2)), (3, lambda: save_dense(2, 2)), (SLOTS, centre_wl),
                         (SLOTS + 1, gain_w1)])

            act.wait_ge(z_saved, SLOTS)
            move_last(act.copy, blocks[9:]).then_inc(z_by_act, 1)
            for j in range(MAXD // P):
                act.wait_ge(*((o_saved, j + 1) if j < KU else (o_done, j + 1)))
                act.activation(o_sq[:, j, :], o_sb[:, j, :] if j < KU else o_ps[j], ACT.Square).then_inc(osq_done, 1)
            act.wait_ge(ovar_done, 1)
            act.activation(o_std[:], ovar_ps, ACT.Sqrt, bias=eps[:, 0:1], scale=1.0 / MAXD).then_inc(ostd_done, 1)
            for j in range(H1 // P):
                act.wait_ge(h1_summed, j + 1)
                act.activation(h1_sb[:, j, :], h1_sum[:, j, :], ACT.Relu).then_inc(h1_ready, 1)
            for j in range(H2 // P):
                act.wait_ge(h2_done, j + 1)
                act.activation(h2_sb[:, j, :], h2_ps[j], ACT.Relu, bias=b2_sb[:, j:j + 1]).then_inc(h2_ready, 1)
            act.wait_ge(top_done, 1)
            act.copy(y_out[:], y_ps).then_inc(y_done, 1)

        @block.vector
        def _(dve):
            links = [0]

            def link(instruction):
                links[0] += 1
                instruction.then_inc(chain, 1)
                dve.wait_ge(chain, links[0])

            def centre(out, in_, mean, width):
                link(dve.tensor_reduce(mean, in_, AX.X, ALU.add))
                link(dve.tensor_scalar(mean, mean, 1.0 / width, None, ALU.mult))
                return dve.tensor_tensor(out, in_, mean.unsqueeze(2).to_broadcast(list(in_.shape)), ALU.subtract)

            dve.wait_ge(ids_in, 32)
            dve.tensor_tensor(rows_sb[:], ids_sb[:], offs_sb[:], ALU.add).then_inc(rows_ready, 1)
            dve.wait_ge(small_in, 16)
            centre(ws_c[:].unsqueeze(1), ws_sb[0:D, :].unsqueeze(1), ws_mean[:], EW).then_inc(prep_dve, 1)
            centre(wsi_c[:].unsqueeze(1), wsi_sb[0:NF, :].unsqueeze(1), wsi_mean[:], PR).then_inc(prep_dve, 1)
            dve.wait_ge(dense_in, 32)
            centre(wd_c[:], wd_sb[:], wd_mean[:], EW).then_inc(prep_dve, 1)
            dve.memset(var_n[:], 1.0)
            dve.wait_ge(mixw_in, 32)
            link(centre(row_w_sb[:], row_w_sb[:], row_w_mean[:], PR))
            wide = [P, TILES, SPAN, PR]
            dve.tensor_tensor(mixw_sb[:], row_w_sb[:].unsqueeze(2).to_broadcast(wide),
                              owner_sb[:].unsqueeze(3).to_broadcast(wide), ALU.mult).then_inc(prep_dve, 1)

            def variance_p(chunk, q):
                s = chunk * QUARTERS + q
                dve.wait_ge(sq_ready, s + 1)
                wait(dve, stdp_ready, s)
                dve.tensor_reduce(var_p[:], y_sq[:], AX.X, ALU.add).then_inc(ssq_ready, 1)

            def variance_n(chunk, q):
                t0, nt = tiles_of(q)
                s = chunk * QUARTERS + q
                dve.wait_ge(quad_done, s + 1)
                wait(dve, std_ready, s)
                dve.wait_ge(gathered[q], chunk * (32 * nt) + 32 * nt)
                dve.tensor_tensor(e_prod[:, 0:2 * nt, :].rearrange("p a d -> p (a d)"), quad_ps[:, 0:P * nt],
                                  e_rows[:, t0:t0 + nt, :].rearrange("p t d -> p (t d)"), ALU.mult).then_inc(prod_done, 1)
                dve.wait_ge(prod_done, s + 1)
                dve.tensor_reduce(var_n[:, 0:2 * nt], e_prod[:, 0:2 * nt, :], AX.X, ALU.add).then_inc(var_ready, 1)

            def norm_p(chunk, q):
                s = chunk * QUARTERS + q
                wide = [P, 2 * QB, PR]
                dve.wait_ge(stdp_ready, s + 1)
                dve.reciprocal(rstd_p[:], std_p[:]).then_inc(rstdp_done, 1)
                dve.wait_ge(rstdp_done, s + 1)
                dve.tensor_tensor(y_a[:], proj_ps[:, q % 2, :, :].rearrange("p a (b q) -> p (a b) q", q=PR),
                                  rstd_p[:].unsqueeze(2).to_broadcast(wide), ALU.mult).then_inc(y_unit, 1)
                dve.wait_ge(y_unit, s + 1)
                dve.tensor_tensor(y_b[:], y_a[:], gsi_sb.unsqueeze(1).to_broadcast(wide), ALU.mult).then_inc(y_gained, 1)
                dve.wait_ge(y_gained, s + 1)
                wait(dve, dotted, s - 1)
                dve.tensor_tensor(feats[:, q % 2, :, 1:PR + 1], y_b[:], bsi_sb.unsqueeze(1).to_broadcast(wide),
                                  ALU.add).then_inc(y_ready, 1)

            def norm_n(chunk, q):
                t0, nt = tiles_of(q)
                s = chunk * QUARTERS + q
                dve.wait_ge(std_ready, s + 1)
                dve.reciprocal(rstd_n[:], std_n[:]).then_inc(rstdn_done, 1)
                dve.wait_ge(rstdn_done, s + 1)
                wait(dve, mixed, s - QUARTERS + 1 + (q < QUARTERS - 1))
                dve.tensor_tensor(e_unit[:, t0:t0 + nt, :].rearrange("p t (a d) -> p (t a) d", d=D),
                                  e_rows[:, t0:t0 + nt, :].rearrange("p t (a d) -> p (t a) d", d=D),
                                  rstd_n[:, 0:2 * nt].unsqueeze(2).to_broadcast([P, 2 * nt, D]),
                                  ALU.mult).then_inc(unit_ready, 1)

            def finish_x():
                dve.wait_ge(prep_act, 7)
                link(dve.reciprocal(x_rstd[:], x_std[:]))
                link(dve.tensor_tensor(x_unit[:], proj_ps[:, 0, 0, :], x_rstd[:], ALU.mult))
                dve.tensor_scalar(x_sb[:], x_unit[:], gd_sb[:, 0:1], bd_sb[:, 0:1], ALU.mult, ALU.add).then_inc(x_ready, 1)
                dve.wait_ge(bl_done, 1)
                dve.tensor_tensor(b1_all[:], bl_ps[:, 0:H1 // P], b1_sb, ALU.add).then_inc(b1_ready, 1)

            def mean_wl():
                dve.wait_ge(wl_in, 16)
                link(dve.tensor_reduce(wl_mean[:], wl_sb[:], AX.X, ALU.add))
                dve.tensor_scalar(wl_mean[:], wl_mean[:], -1.0 / MAXD, None, ALU.mult).then_inc(wl_mean_ready, 1)

            slots(dve, [(3, variance_p), (1, variance_n), (3, norm_p), (1, norm_n)],
                  extra=[(1, finish_x), (3, mean_wl)])

            dve.wait_ge(z_saved, SLOTS)
            move_last(dve.tensor_copy, blocks[:9]).then_inc(z_by_dve, 1)
            for c in range(KU):
                dve.wait_ge(o_done, c + 1)
                dve.tensor_copy(o_sb[:, c, :], o_ps[c]).then_inc(o_saved, 1)
            dve.wait_ge(ostd_done, 1)
            link(dve.reciprocal(o_rstd[:], o_std[:]))
            for j in range(H1 // P):
                dve.wait_ge(h1_done, j + 1)
                link(dve.tensor_tensor(h1_unit[:, j, :], h1_ps[j], o_rstd[:], ALU.mult))
                dve.tensor_tensor(h1_sum[:, j, :], h1_unit[:, j, :], h1_dense[:, j, :], ALU.add).then_inc(h1_summed, 1)


def kernel(**inputs):
    import concourse.bacc as bacc
    from concourse.bass_utils import run_bass_kernel_spmd

    a = {k: np.asarray(v) for k, v in inputs.items()}

    def by_partition(m):
        return np.ascontiguousarray(m.reshape(-1, P, m.shape[1]).transpose(1, 0, 2))

    def columns(v):
        return np.ascontiguousarray(v.reshape(-1, P).T)

    order = np.arange(B).reshape(CHUNKS, 2, QUARTERS, QB // 4, 4).transpose(0, 4, 2, 1, 3).reshape(-1)
    small = np.zeros((P, PACKED), np.float32)

    def put(name, v):
        begin, end = PACK[name]
        small[:v.shape[0], begin:end] = v

    put("eye", np.eye(P, dtype=np.float32))
    put("ws", np.concatenate([a["L0_rec_Ws"].T, a["L0_rec_bs"][None]]))
    put("wsi", a["L0_rec_Wsi"].T)
    put("gsi", np.broadcast_to(a["L0_rec_gsi"], (P, PR)))
    put("bsi", np.broadcast_to(a["L0_rec_bsi"], (P, PR)))
    put("gs", columns(a["L0_rec_gs"]))
    put("gd", columns(a["L0_rec_gd"]))
    put("bd", columns(a["L0_rec_bd"]))
    put("gl", columns(a["L0_rec_gl"][:USED]))
    put("bl", columns(a["L0_rec_bl"][:USED]))
    put("b1", columns(a["b_top1"]))
    put("b2", columns(a["b_top2"]))
    put("w3", columns(a["W_top3"][:, 0]))

    row = np.arange(TILES * P).reshape(TILES, P)
    sample, feature = row // NF, row % NF
    starts = np.concatenate([[0], np.cumsum(VOCAB)[:-1]]).astype(np.int32)
    offs = np.broadcast_to(starts[feature].T[:, None, :, None], (P, CHUNKS, TILES, 2)).reshape(P, -1)
    ids = a["ids"].reshape(CHUNKS, 2, TILES, P).transpose(3, 0, 2, 1).reshape(P, -1)
    row_w = a["L0_rec_Wsi"].T[feature].transpose(1, 0, 2)
    first = np.array([first_sample(t) for t in range(TILES)])[:, None]
    owner = ((sample - first)[:, :, None] == np.arange(SPAN)).astype(np.float32).transpose(1, 0, 2)
    wl = np.zeros((4, PR, KZ, MAXD), np.float32)
    for c in range(PR):
        for p in range(c, PR):
            wl[c // KZ, p, c % KZ] = a["L0_rec_Wl"][:, (p + 1) * p // 2 + c]
    w1 = a["W_top1"]
    arrays = {
        "table": np.concatenate([a[f"tbl_{n}"] for n in range(NF)]),
        "ids": np.ascontiguousarray(ids),
        "offs": np.ascontiguousarray(offs),
        "small": small,
        "row_w": np.ascontiguousarray(row_w),
        "owner": np.ascontiguousarray(owner),
        "dense_t": by_partition(np.ascontiguousarray(a["r_dense_t"][order].T)),
        "wd_t": by_partition(np.ascontiguousarray(a["L0_rec_Wd"].T)),
        "wl": wl.reshape(P, KZ, MAXD),
        "w1": by_partition(np.concatenate([w1[:USED], w1[MAXD:]])),
        "w2": by_partition(a["W_top2"]),
    }
    nc = bacc.Bacc("TRN2", target_bir_lowering=False, num_devices=1)
    args = [nc.dram_tensor(f"{name}_dram", v.shape, mybir.dt.from_np(v.dtype), kind="ExternalInput").ap()
            for name, v in arrays.items()]
    args.append(nc.dram_tensor("out_dram", (1, B), F32, kind="ExternalOutput").ap())
    tower(nc, *args)
    r = run_bass_kernel_spmd(nc, [{f"{name}_dram": v for name, v in arrays.items()}], core_ids=[0])
    y = np.empty((B, 1), np.float32)
    y[order, 0] = r.results[0]["out_dram"][0]
    return y
```

```python
from contextlib import ExitStack

import numpy as np

import concourse.bass as bass
from concourse import mybir

ALU = mybir.AluOpType
ACT = mybir.ActivationFunctionType
AX = mybir.AxisListType
F32 = mybir.dt.float32
I32 = mybir.dt.int32

P = 128
VOCAB = [1000, 125000, 1000, 12500, 12500, 12500, 1000, 12500, 1000, 1250, 125000, 1250, 1250, 1000,
         1000, 1250, 1000, 1250, 125000, 1000, 1250, 1000, 12500, 1000, 1000, 1000]
NF = len(VOCAB)
D = 64
EW = 128
PR = 32
B = 512
CHUNKS = B // P
HALF = P // 2
TILES = HALF * NF // P
QUARTERS = 4
QB = HALF // QUARTERS
SLOTS = CHUNKS * QUARTERS
SPAN = 6
MAXD = 512
USED = 384
DENSE = 256
H1 = 512
H2 = 256
BANDS = 4
BAND = PR // BANDS
MOMENTS = PR + 2
KU = USED // P
KD = DENSE // P
EPS = 1e-5


def pair_pieces():
    pieces, at = [], 0
    for band in (0, 1, 3, 2):
        pair, end = BAND * BAND * band, PR * BAND
        while pair < end:
            number = min(end - pair, P - at % P)
            pieces.append((at // P, at % P, band, pair, number))
            at, pair = at + number, pair + number
    assert at % P == 0
    return pieces


PIECES = pair_pieces()
KZ = PIECES[-1][0] + 1
MOVES = 16 * (len(PIECES) + 1)


def first_sample(t):
    return P * t // NF


def tiles_of(q):
    end = [-(-(q1 + 1) * QB * NF // P) for q1 in range(QUARTERS)]
    begin = end[q - 1] if q else 0
    return begin, end[q] - begin


def mix_parts(q):
    parts = []
    for t in range(TILES):
        lo = max(q * QB, first_sample(t))
        hi = min((q + 1) * QB, (P * (t + 1) - 1) // NF + 1)
        if lo < hi:
            parts.append((t, lo - first_sample(t), lo - q * QB, hi - lo))
    return parts


PACK = {}
for _name, _width in (("eye", P), ("ws", EW), ("wsi", PR), ("gs", 1), ("gd", 1), ("bd", 1),
                      ("gl", USED // P), ("bl", USED // P), ("b1", H1 // P), ("b2", H2 // P), ("w3", H2 // P)):
    _at = max([end for _, end in PACK.values()], default=0)
    PACK[_name] = (_at, _at + _width)
PACKED = max(end for _, end in PACK.values())


PAIR_PACK = {}
for _name, _width in (("gsi_p", KZ), ("gsi_c", KZ), ("bsi_p", KZ), ("bsi_c", KZ), ("gsi_m", 1), ("is_p", KZ * MOMENTS),
                      ("is_c", KZ * MOMENTS)):
    _at = max([end for _, end in PAIR_PACK.values()], default=0)
    PAIR_PACK[_name] = (_at, _at + _width)
PAIR_COLUMNS = max(end for _, end in PAIR_PACK.values())


def tower(nc, table, ids, offs, small, row_w, owner, dense_t, wd_t, pairs, wl, w1, w2, z_dram, s_dram, out):
    with ExitStack() as ctx:
        def sb(name, shape, dt=F32):
            return ctx.enter_context(nc.sbuf_tensor(name, shape, dt))

        def psum(name, shape):
            return ctx.enter_context(nc.psum_tensor(name, shape, F32))

        def sem(name):
            return ctx.enter_context(nc.semaphore(name))

        turn_ps = psum("turn_ps", [P, 512])
        quad_ps = psum("quad_ps", [P, 512])
        mix_ps = psum("mix_ps", [P, 512])
        dots_ps = psum("dots_ps", [P, 512])
        proj_ps = psum("proj_ps", [P, 2, 512])
        o_ps = psum("o_ps", [P, 512])
        o_turn_ps = psum("o_turn_ps", [P, 512])

        dense_ps = [o_ps[:], o_turn_ps[:], dots_ps[:], mix_ps[:]]
        bl_ps = o_turn_ps
        xsum_ps = proj_ps[:, 1, :]
        moment_ps = o_ps[0:MOMENTS, :]
        o_last_ps = turn_ps
        h1_ps = [quad_ps[:], mix_ps[:], proj_ps[:, 0, :], proj_ps[:, 1, :]]
        h2_ps = [o_ps[:], dots_ps[:]]
        h2_last_ps = o_turn_ps
        y_ps = turn_ps[:, 0:CHUNKS]

        ids_sb = sb("ids_sb", [P, CHUNKS * TILES * 2], I32)
        offs_sb = sb("offs_sb", [P, CHUNKS * TILES * 2], I32)
        rows_sb = sb("rows_sb", [P, CHUNKS * TILES * 2], I32)
        e_rows = sb("e_rows", [P, TILES, 2 * D])
        e_unit = sb("e_unit", [P, TILES, 2 * D])
        e_cols = sb("e_cols", [P, 2, 4 * P])
        e_prod = sb("e_prod", [P, 4 * 2, D])
        var_n = sb("var_n", [P, 8])
        std_n = sb("std_n", [P, 8])
        rstd_n = sb("rstd_n", [P, 8])
        f_sb = sb("f_sb", [P, 2, 2, 512])
        y_sq = sb("y_sq", [P, 2 * QB, PR])
        var_p = sb("var_p", [P, 2 * QB])
        std_p = sb("std_p", [P, 2 * QB])
        rstd_p = sb("rstd_p", [P, 2 * QB])
        feats = sb("feats", [P, 2, 2 * QB, PR + 2])
        z_mine = sb("z_mine", [P, CHUNKS, PR + 1, PR])
        moments = sb("moments", [MOMENTS, CHUNKS, 4, PR])
        z_pairs = sb("z_pairs", [P, KZ, 4, PR])
        moment_cols = sb("moment_cols", [MOMENTS, P])
        z_last = sb("z_last", [P, KZ, 4, PR])
        moment_last = sb("moment_last", [MOMENTS, P])

        small_sb = sb("small_sb", [P, PACKED])
        eye_sb, ws_sb, wsi_sb, gs_sb, gd_sb, bd_sb, gl_sb, bl_sb, b1_sb, b2_sb, w3_sb = (
            small_sb[:, begin:end] for begin, end in PACK.values())
        pairs_sb = sb("pairs_sb", [P, PAIR_COLUMNS])
        gsi_p, gsi_c, bsi_p, bsi_c, gsi_m, is_p, is_c = (pairs_sb[:, begin:end] for begin, end in PAIR_PACK.values())
        wl_gain = sb("wl_gain", [P, KZ])
        wl_bias = sb("wl_bias", [P, KZ])
        pick_p = sb("pick_p", [P, KZ, MOMENTS])
        pick_c = sb("pick_c", [P, KZ, MOMENTS])
        pick = sb("pick", [P, KZ, MOMENTS])
        one_w = sb("one_w", [P, KZ])
        moment_w = sb("moment_w", [MOMENTS, MAXD])
        moment_mean = sb("moment_mean", [MOMENTS, 1])
        ones = sb("ones", [P, P])
        eps = sb("eps", [P, 1])
        mixw_sb = sb("mixw_sb", [P, TILES, SPAN, PR])
        row_w_sb = sb("row_w_sb", [P, TILES, PR])
        row_w_mean = sb("row_w_mean", [P, TILES])
        owner_sb = sb("owner_sb", [P, TILES, SPAN])
        wsi_mean = sb("wsi_mean", [NF, 1])
        wsi_c = sb("wsi_c", [NF, PR])
        ws_mean = sb("ws_mean", [D, 1])
        ws_c = sb("ws_c", [D, EW])
        ws_rows = sb("ws_rows", [EW, 2, D])
        ws_grows = sb("ws_grows", [EW, D])
        gram = sb("gram", [P, P])
        proj_w = sb("proj_w", [P, EW])
        dense_sb = sb("dense_sb", [P, KD, B])
        wd_sb = sb("wd_sb", [P, KD, EW])
        wd_mean = sb("wd_mean", [P, KD])
        wd_c = sb("wd_c", [P, KD, EW])
        x_sq = sb("x_sq", [P, B])
        x_std = sb("x_std", [P, B])
        x_rstd = sb("x_rstd", [P, B])
        x_unit = sb("x_unit", [P, B])
        x_sb = sb("x_sb", [P, B])
        wl_sb = sb("wl_sb", [P, KZ, MAXD])
        wl_mean = sb("wl_mean", [P, KZ])
        w1_sb = sb("w1_sb", [P, KU + KD, H1])
        w1_g = sb("w1_g", [P, KU, H1])
        b1_all = sb("b1_all", [P, H1 // P])
        w2_sb = sb("w2_sb", [P, H1 // P, H2])
        o_sq = sb("o_sq", [P, MAXD])
        o_var = sb("o_var", [P, 1])
        o_std = sb("o_std", [P, 1])
        o_rstd = sb("o_rstd", [P, 1])
        o_unit = sb("o_unit", [P, USED])
        o_sb = sb("o_sb", [P, KU, B])
        h1_dense = sb("h1_dense", [P, H1 // P, B])
        h1_sb = sb("h1_sb", [P, H1 // P, B])
        h2_sb = sb("h2_sb", [P, H2 // P, B])
        y_out = sb("y_out", [P, CHUNKS])

        ids_in, small_in, mixw_in, dense_in = sem("ids_in"), sem("small_in"), sem("mixw_in"), sem("dense_in")
        w1_in, wl_in, w2_in, out_done = sem("w1_in"), sem("wl_in"), sem("w2_in"), sem("out_done")
        pairs_in, w1_dense_in = sem("pairs_in"), sem("w1_dense_in")
        gathered = [sem(f"gathered{q}") for q in range(QUARTERS)]
        rows_ready = sem("rows_ready")
        consts = sem("consts")
        prep_dve, prep_pe, prep_act = sem("prep_dve"), sem("prep_pe"), sem("prep_act")
        turned, cols_ready, quad_done, var_ready, std_ready, unit_ready = (
            sem(n) for n in ("turned", "cols_ready", "quad_done", "var_ready", "std_ready", "unit_ready"))
        mixed, f_ready, projected, sq_ready, ssq_ready, stdp_ready = (
            sem(n) for n in ("mixed", "f_ready", "projected", "sq_ready", "ssq_ready", "stdp_ready"))
        y_ready, x_placed, dotted, z_saved, z_moved, z_last_moved = (
            sem(n) for n in ("y_ready", "x_placed", "dotted", "z_saved", "z_moved", "z_last_moved"))
        chain = sem("chain")
        prod_done, rstdn_done, rstdp_done = (sem(n) for n in ("prod_done", "rstdn_done", "rstdp_done"))
        xsum_done, xsum_saved, pick_ready, moment_done, moment_saved, moment_ready = (
            sem(n) for n in ("xsum_done", "xsum_saved", "pick_ready", "moment_done", "moment_saved", "moment_ready"))
        o_done, osq_done, ovar_done, ostd_done, orstd_done, o_scaled, o_turned, o_saved, x_ready, moments_ready = (
            sem(n) for n in ("o_done", "osq_done", "ovar_done", "ostd_done", "orstd_done", "o_scaled", "o_turned",
                             "o_saved", "x_ready", "moments_ready"))
        wl_summed, z_out = sem("wl_summed"), sem("z_out")
        bl_done, b1_ready, dense_done, dense_saved, wl_mean_ready, wl_ready, w1_ready, h1_summed = (
            sem(n) for n in ("bl_done", "b1_ready", "dense_done", "dense_saved", "wl_mean_ready", "wl_ready",
                             "w1_ready", "h1_summed"))
        h1_done, h1_ready, h2_done, h2_ready, top_done, y_done = (
            sem(n) for n in ("h1_done", "h1_ready", "h2_done", "h2_ready", "top_done", "y_done"))

        block = ctx.enter_context(nc.Block())

        def slots(eng, stages, extra=()):
            latest = max(late for late, _ in stages)

            def slot(chunk, q, s=None):
                for late, stage in stages:
                    if s is None or 0 <= s - late < SLOTS:
                        stage(chunk + (q - late) // QUARTERS, (q - late) % QUARTERS)
                for after, work in extra:
                    if s == after:
                        work()

            peeled = -(-latest // QUARTERS) * QUARTERS
            for s in range(peeled):
                slot(s // QUARTERS, s % QUARTERS, s)
            with eng.Fori(peeled // QUARTERS, CHUNKS) as chunk:
                for q in range(QUARTERS):
                    slot(chunk, q)
            for s in range(SLOTS, SLOTS + latest):
                slot(s // QUARTERS, s % QUARTERS, s)

        def wait(eng, semaphore, count):
            if not isinstance(count, int) or count > 0:
                eng.wait_ge(semaphore, count)

        def with_last(stage):
            def of_chunk(chunk, q):
                if q == QUARTERS - 1:
                    stage(chunk)
            return of_chunk

        def is_last(chunk):
            return isinstance(chunk, int) and chunk == CHUNKS - 1

        def in_loop(stage):
            return with_last(lambda chunk: None if isinstance(chunk, int) else stage(chunk))

        @block.sync
        def _(sp):
            sp.dma_start(ids_sb[:], ids).then_inc(ids_in, 16)
            sp.dma_start(offs_sb[:], offs).then_inc(ids_in, 16)
            sp.dma_start(small_sb[:], small).then_inc(small_in, 16)
            sp.dma_start(wd_sb[:], wd_t).then_inc(dense_in, 16)
            sp.dma_start(dense_sb[:], dense_t).then_inc(dense_in, 16)
            sp.dma_start(w1_sb[:, KU:KU + KD, :], w1[:, KU:KU + KD, :]).then_inc(w1_dense_in, 16)
            sp.dma_start(row_w_sb[:], row_w).then_inc(mixw_in, 16)
            sp.dma_start(owner_sb[:], owner).then_inc(mixw_in, 16)
            sp.dma_start(pairs_sb[:], pairs).then_inc(pairs_in, 16)
            sp.wait_ge(gathered[0], 32 * tiles_of(0)[1])
            sp.dma_start(w1_sb[:, 0:KU, :], w1[:, 0:KU, :]).then_inc(w1_in, 16)
            for q in range(1, QUARTERS):
                sp.wait_ge(gathered[q], 32 * tiles_of(q)[1])
                begin, end = (q - 1) * KZ // 3, q * KZ // 3
                sp.dma_start(wl_sb[:, begin:end, :], wl[:, begin:end, :]).then_inc(wl_in, 16)
            sp.dma_start(w2_sb[:], w2).then_inc(w2_in, 16)
            def write_z(chunk):
                sp.wait_ge(z_saved, chunk * QUARTERS + QUARTERS)
                mine = z_mine[:, bass.ds(chunk, 1), :, :]
                sp.dma_start(z_dram[bass.ds(chunk, 1), :, :, :].rearrange("s b p n -> p (s b) n"),
                             mine[:, :, 1:PR + 1, :].rearrange("p s (b c) g -> p (s b) (c g)", b=BANDS)).then_inc(z_out, 16)
                sp.dma_start(s_dram[bass.ds(chunk, 1), :, :].rearrange("s p g -> p (s g)"),
                             mine[:, :, 0, :].rearrange("p s g -> p (s g)")).then_inc(z_out, 16)
                sp.wait_ge(z_out, chunk * 32 + 32)

            def read_z(chunk, pairs_on_rows, semaphore):
                for t, row, band, pair, number in PIECES:
                    sp.dma_start(pairs_on_rows[row:row + number, t, :, :],
                                 z_dram[bass.ds(chunk, 1), band, :, :].rearrange(
                                     "s (k p) (c g) -> (s p c) k g", k=4, g=PR)[pair:pair + number, :, :]
                                 ).then_inc(semaphore, 16)
                sp.dma_start(moments[0:PR, bass.ds(chunk, 1), :, :].rearrange("p s k g -> p (s k) g"),
                             s_dram[bass.ds(chunk, 1), :, :].rearrange("s (k p) g -> p (s k) g", k=4)
                             ).then_inc(semaphore, 16)

            write_z(0)
            read_z(0, z_pairs, z_moved)
            with sp.Fori(1, CHUNKS - 1) as chunk:
                write_z(chunk)
                sp.wait_ge(o_done, chunk)
                sp.wait_ge(moments_ready, chunk)
                read_z(chunk, z_pairs, z_moved)
            write_z(CHUNKS - 1)
            read_z(CHUNKS - 1, z_last, z_last_moved)
            sp.wait_ge(y_done, 1)
            sp.dma_start(out, y_out[:]).then_inc(out_done, 16)
            sp.wait_ge(out_done, 16)

        @block.gpsimd
        def _(pool):
            pool.memset(ones[:], 1.0).then_inc(consts, 1)
            pool.memset(eps[:], EPS).then_inc(consts, 1)
            pool.memset(gram[:], 0.0).then_inc(consts, 1)
            pool.memset(proj_w[:], 0.0).then_inc(consts, 1)
            pool.memset(feats[:, :, :, 0], 1.0).then_inc(consts, 1)
            pool.wait_ge(rows_ready, 1)
            for chunk in range(CHUNKS):
                for q in range(QUARTERS):
                    wait(pool, unit_ready, QUARTERS * (chunk - 1) + q + 1)
                    t0, nt = tiles_of(q)
                    for t in range(t0, t0 + nt):
                        for ab in range(2):
                            col = (chunk * TILES + t) * 2 + ab
                            pool.indirect_dma_start(
                                out=e_rows[:, t, D * ab:D * (ab + 1)], out_offset=None, in_=table,
                                in_offset=bass.IndirectOffsetOnAxis(ap=rows_sb[:, col:col + 1], axis=0),
                            ).then_inc(gathered[q], 16)

        @block.tensor
        def _(pe):
            pe.wait_ge(small_in, 16)
            pe.wait_ge(consts, 5)
            pe.wait_ge(prep_dve, 2)
            pe.matmul(quad_ps[:, 0:PR], ones[0:NF, :], wsi_c[:], start=True, stop=True).then_inc(prep_pe, 1)
            pe.transpose(turn_ps[:, 0:D], ws_c[:], eye_sb[0:D, 0:D]).then_inc(prep_pe, 1)
            pe.wait_ge(prep_act, 2)
            pe.matmul(mix_ps[:, 0:D], ws_rows[:].rearrange("p a d -> p (a d)"), ws_rows[:, 0, :], start=True,
                      stop=True).then_inc(prep_pe, 1)
            pe.wait_ge(prep_act, 3)
            pe.transpose(dots_ps[0:D, 0:EW], ws_grows[:], eye_sb).then_inc(prep_pe, 1)
            pe.wait_ge(dense_in, 32)
            pe.wait_ge(prep_dve, 3)
            for j in range(KD):
                mm = pe.matmul(proj_ps[:, 0, :], wd_c[:, j, :], dense_sb[:, j, :], start=(j == 0), stop=(j == KD - 1))
            mm.then_inc(prep_pe, 1)
            def top_dense(j):
                for c in range(KD):
                    mm = pe.matmul(dense_ps[j], w1_sb[:, KU + c, P * j:P * (j + 1)], dense_sb[:, c, :],
                                   start=(c == 0), stop=(c == KD - 1))
                mm.then_inc(dense_done, 1)

            pe.wait_ge(w1_dense_in, 16)
            top_dense(0)
            pe.wait_ge(prep_act, 6)
            pe.matmul(proj_ps[:, 1, :], ones[:], x_sq[:], start=True, stop=True).then_inc(prep_pe, 1)
            for j in range(1, H1 // P):
                top_dense(j)

            def sum_x():
                pe.wait_ge(x_ready, 1)
                pe.matmul(xsum_ps, ones[:], x_sb[:], start=True, stop=True).then_inc(xsum_done, 1)
                pe.wait_ge(dense_saved, H1 // P)

            def top_bl():
                pe.wait_ge(w1_in, 16)
                for j in range(H1 // P):
                    for c in range(KU):
                        mm = pe.matmul(bl_ps[:, j:j + 1], w1_sb[:, c, P * j:P * (j + 1)], bl_sb[:, c:c + 1],
                                       start=(c == 0), stop=(c == KU - 1))
                mm.then_inc(bl_done, 1)
                pe.wait_ge(xsum_saved, 1)

            def weigh_moments(first, number):
                pe.wait_ge(wl_in, 16 * 3)
                pe.wait_ge(pick_ready, 1)
                for c in range(first, first + number):
                    mm = pe.matmul(moment_ps, pick[:, c, :], wl_sb[:, c, :], start=(c == 0), stop=(c == KZ - 1))
                if first + number == KZ:
                    mm.then_inc(moment_done, 1)

            def turn(chunk, q):
                t0, nt = tiles_of(q)
                s = chunk * QUARTERS + q
                pe.wait_ge(gathered[q], chunk * (32 * nt) + 32 * nt)
                wait(pe, cols_ready, s)
                for t in range(nt):
                    mm = pe.transpose(turn_ps[:, P * t:P * (t + 1)], e_rows[:, t0 + t, :], eye_sb)
                mm.then_inc(turned, 1)

            def mix(chunk, q):
                s = chunk * QUARTERS + q
                pe.wait_ge(unit_ready, s + 1)
                wait(pe, f_ready, 2 * s)
                for n, (t, lo, at, number) in enumerate(mix_parts(q)):
                    mm = pe.matmul(mix_ps[:, PR * at:PR * (at + number)], e_unit[:, t, :],
                                   mixw_sb[:, t, lo:lo + number, :].rearrange("k b p -> k (b p)"),
                                   start=(n == 0), stop=(n == len(mix_parts(q)) - 1), skip_group_check=True)
                mm.then_inc(mixed, 1)

            def quad(chunk, q):
                _, nt = tiles_of(q)
                s = chunk * QUARTERS + q
                pe.wait_ge(cols_ready, s + 1)
                wait(pe, var_ready, s)
                for t in range(nt):
                    mm = pe.matmul(quad_ps[:, P * t:P * (t + 1)], e_cols[:, q % 2, P * t:P * (t + 1)], gram[:],
                                   start=True, stop=True)
                mm.then_inc(quad_done, 1)

            def dots(chunk, q):
                s = chunk * QUARTERS + q
                pe.wait_ge(y_ready, 2 * s + 2)
                pe.wait_ge(x_placed, s + 1)
                wait(pe, z_saved, s)
                for g in range(2 * QB // 4):
                    for k in range(4):
                        f = feats[:, q % 2, 4 * g + k, :]
                        mm = pe.matmul(dots_ps[PR * k:PR * (k + 1), (PR + 1) * g:(PR + 1) * (g + 1)], f[:, 2:PR + 2],
                                       f[:, 0:PR + 1], start=True, stop=True)
                mm.then_inc(dotted, 1)

            def project(chunk, q):
                s = chunk * QUARTERS + q
                for ab in range(2):
                    wait(pe, y_ready, 2 * s - 1 + ab)
                    pe.wait_ge(f_ready, 2 * s + ab + 1)
                    pe.matmul(proj_ps[:, ab, :], proj_w[:], f_sb[:, q % 2, ab, :], start=True,
                              stop=True).then_inc(projected, 1)
                if isinstance(s, int) and s == SLOTS - 2:
                    top_1_early()

            def linear(chunk, part=range(KZ + 1)):
                pe.wait_ge(wl_ready, KZ)
                pe.wait_ge(moment_ready, 1)
                if is_last(chunk):
                    pairs_on_rows, moments_on_rows, bank = z_last, moment_last, o_last_ps
                    pe.wait_ge(z_last_moved, MOVES)
                    pe.wait_ge(cols_ready, SLOTS)
                else:
                    pairs_on_rows, moments_on_rows, bank = z_pairs, moment_cols, o_ps
                    pe.wait_ge(z_moved, chunk * MOVES + MOVES)
                    wait(pe, o_scaled, chunk)
                for c in part:
                    if c < KZ:
                        pe.matmul(bank[:], pairs_on_rows[:, c, :, :].rearrange("p k g -> p (k g)"), wl_sb[:, c, :],
                                  start=(c == 0), stop=False)
                    else:
                        pe.wait_ge(moments_ready, chunk + 1)
                        pe.matmul(bank[:], moments_on_rows[:], moment_w[:], start=False, stop=True).then_inc(o_done, 1)

            def turn_o(chunk):
                pe.wait_ge(o_scaled, chunk + 1)
                wait(pe, o_saved, chunk)
                for j in range(KU):
                    mm = pe.transpose(o_turn_ps[:, P * j:P * (j + 1)], o_unit[:, P * j:P * (j + 1)], eye_sb)
                mm.then_inc(o_turned, 1)

            def top_1(j, first, number):
                for c in range(KU):
                    mm = pe.matmul(h1_ps[j][:, P * first:P * (first + number)], w1_g[:, c, P * j:P * (j + 1)],
                                   o_sb[:, c, P * first:P * (first + number)], start=(c == 0), stop=(c == KU - 1))
                return mm

            def top_1_early():
                pe.wait_ge(w1_ready, 1)
                pe.wait_ge(o_saved, CHUNKS - 2)
                pe.wait_ge(var_ready, SLOTS)
                top_1(0, 0, CHUNKS - 2)

            slots(pe, [(3, project), (1, quad), (0, turn), (2, mix), (4, dots), (8, in_loop(turn_o)), (7, in_loop(linear))],
                  extra=[(1, sum_x), (1, top_bl), (3, lambda: weigh_moments(0, 3)),
                         (4, lambda: weigh_moments(3, KZ - 3)), (SLOTS + 2, lambda: linear(CHUNKS - 2, range(0, 3)))])

            pe.wait_ge(w1_ready, 1)
            pe.wait_ge(w2_in, 16)
            pe.wait_ge(o_saved, CHUNKS - 2)
            linear(CHUNKS - 2, range(3, KZ + 1))
            for j in range(1, H1 // P - 1):
                top_1(j, 0, CHUNKS - 2)
            turn_o(CHUNKS - 2)
            top_1(H1 // P - 1, 0, CHUNKS - 2)
            pe.wait_ge(o_saved, CHUNKS - 1)
            for j in range(H1 // P):
                top_1(j, CHUNKS - 2, 1).then_inc(h1_done, 1)
            linear(CHUNKS - 1)

            def top_2(first, number, turn, part=range(H1 // P)):
                for c in part:
                    pe.wait_ge(h1_ready, H1 // P * turn + c + 1)
                    for j in range(H2 // P):
                        to = (h2_last_ps[:, P * j:P * (j + 1)] if turn else h2_ps[j][:, P * first:P * (first + number)])
                        mm = pe.matmul(to, w2_sb[:, c, P * j:P * (j + 1)],
                                       h1_sb[:, c, P * first:P * (first + number)],
                                       start=(c == 0 and not (turn and j)),
                                       stop=(c == H1 // P - 1), skip_group_check=True)
                        if c == H1 // P - 1:
                            mm.then_inc(h2_done, 1)

            def top_3(first, number, turn):
                pe.wait_ge(h2_ready, H2 // P * (turn + 1))
                for chunk in range(first, first + number):
                    for c in range(H2 // P):
                        mm = pe.matmul(y_ps[:, chunk:chunk + 1], h2_sb[:, c, P * chunk:P * (chunk + 1)], w3_sb[:, c:c + 1],
                                       start=(c == 0), stop=(c == H2 // P - 1))
                return mm

            pe.wait_ge(z_saved, SLOTS)
            top_2(0, CHUNKS - 1, 0, range(0, 2))
            turn_o(CHUNKS - 1)
            top_2(0, CHUNKS - 1, 0, range(2, 3))
            pe.wait_ge(o_saved, CHUNKS)
            for j in range(H1 // P):
                top_1(j, CHUNKS - 1, 1).then_inc(h1_done, 1)
            top_2(0, CHUNKS - 1, 0, range(3, 4))
            top_2(CHUNKS - 1, 1, 1)
            top_3(0, CHUNKS - 1, 0)
            top_3(CHUNKS - 1, 1, 1).then_inc(top_done, 1)

        @block.scalar
        def _(act):
            act.wait_ge(consts, 5)
            act.activation(x_std[:, 0:1], eps[:, 0:1], ACT.Sqrt)
            act.wait_ge(small_in, 16)
            act.wait_ge(prep_pe, 1)
            for half in range(2):
                for ab in range(2):
                    last = act.copy(f_sb[D:P, half, ab, :].rearrange("p (b q) -> p b q", q=PR),
                                    quad_ps[D:P, 0:PR].unsqueeze(1).to_broadcast([P - D, QB, PR]))
            last.then_inc(prep_act, 1)
            act.wait_ge(prep_pe, 2)
            act.copy(ws_rows[:], turn_ps[:, 0:D].unsqueeze(1).to_broadcast([P, 2, D])).then_inc(prep_act, 1)
            act.activation(ws_grows[:], turn_ps[:, 0:D], ACT.Copy, scale=gs_sb[:, 0:1]).then_inc(prep_act, 1)
            act.wait_ge(prep_pe, 3)
            act.copy(gram[0:D, 0:D], mix_ps[0:D, 0:D])
            act.copy(gram[D:P, D:P], mix_ps[D:P, 0:D]).then_inc(prep_act, 1)
            act.wait_ge(prep_pe, 4)
            act.copy(proj_w[D:D + 1, :], ws_sb[D:D + 1, :])
            act.copy(proj_w[0:D, :], dots_ps[0:D, 0:EW]).then_inc(prep_act, 1)
            act.wait_ge(prep_pe, 5)
            act.activation(x_sq[:], proj_ps[:, 0, :], ACT.Square).then_inc(prep_act, 1)
            act.wait_ge(prep_pe, 6)
            act.activation(x_std[:], proj_ps[:, 1, :], ACT.Sqrt, bias=eps[:, 0:1], scale=1.0 / EW).then_inc(prep_act, 1)
            for j in range(H1 // P):
                act.wait_ge(dense_done, j + 1)
                act.copy(h1_dense[:, j, :], dense_ps[j]).then_inc(dense_saved, 1)

            def square(chunk, q):
                s = chunk * QUARTERS + q
                wait(act, ssq_ready, s)
                for ab in range(2):
                    act.wait_ge(projected, 2 * s + ab + 1)
                    act.activation(y_sq[:, QB * ab:QB * (ab + 1), :].rearrange("p b q -> p (b q)"),
                                   proj_ps[:, ab, :], ACT.Square).then_inc(sq_ready, 1)

            def save_cols(chunk, q):
                _, nt = tiles_of(q)
                s = chunk * QUARTERS + q
                act.wait_ge(turned, s + 1)
                wait(act, quad_done, s - 1)
                act.copy(e_cols[:, q % 2, 0:P * nt], turn_ps[:, 0:P * nt]).then_inc(cols_ready, 1)

            def save_f(chunk, q):
                s = chunk * QUARTERS + q
                act.wait_ge(mixed, s + 1)
                wait(act, projected, 2 * s - 2)
                for ab in range(2):
                    act.copy(f_sb[0:D, q % 2, ab, :], mix_ps[D * ab:D * (ab + 1), :]).then_inc(f_ready, 1)

            def root_n(chunk, q):
                s = chunk * QUARTERS + q
                act.wait_ge(var_ready, s + 1)
                act.activation(std_n[:], var_n[:], ACT.Sqrt, bias=eps[:, 0:1], scale=1.0 / EW).then_inc(std_ready, 1)

            def root_p(chunk, q):
                s = chunk * QUARTERS + q
                act.wait_ge(ssq_ready, s + 1)
                act.activation(std_p[:], var_p[:], ACT.Sqrt, bias=eps[:, 0:1], scale=1.0 / PR).then_inc(stdp_ready, 1)

            def place_x(chunk, q):
                s = chunk * QUARTERS + q
                act.wait_ge(x_ready, 1)
                wait(act, dotted, s - 1)
                x = x_sb[:].rearrange("p (s k q a i) -> p s k q a i", s=CHUNKS, k=4, q=QUARTERS, a=2)
                for ab in range(2):
                    src = x[:, bass.ds(chunk, 1), :, q, ab, :].rearrange("p s k i -> p (s i) k")
                    last = act.copy(feats[:, q % 2, QB * ab:QB * (ab + 1), 1].rearrange("p (i k) -> p i k", k=4), src)
                last.then_inc(x_placed, 1)

            def save_z(chunk, q):
                s = chunk * QUARTERS + q
                act.wait_ge(dotted, s + 1)
                n = 2 * QB // 4
                act.copy(z_mine[:, bass.ds(chunk, 1), :, n * q:n * (q + 1)].rearrange("p s c g -> p (s c) g"),
                         dots_ps[:, 0:(PR + 1) * n].rearrange("p (g c) -> p c g", c=PR + 1)).then_inc(z_saved, 1)

            def save_xsum():
                act.wait_ge(xsum_done, 1)
                act.copy(moments[PR:PR + 1, :, :, :].rearrange("p s k g -> p (s k g)"),
                         xsum_ps[PR:PR + 1, :]).then_inc(xsum_saved, 1)

            def save_moment_w():
                act.wait_ge(moment_done, 1)
                act.activation(moment_w[:], moment_ps, ACT.Copy, scale=gsi_m[0:MOMENTS, :]).then_inc(moment_saved, 1)

            def gain_wl(first, number):
                act.wait_ge(wl_mean_ready, 1)
                act.wait_ge(moment_done, 1)
                for c in range(first, first + number):
                    act.activation(wl_sb[:, c, :], wl_sb[:, c, :], ACT.Identity, bias=wl_bias[:, c:c + 1],
                                   scale=wl_gain[:, c:c + 1]).then_inc(wl_ready, 1)

            def gain_w1():
                act.wait_ge(w1_in, 16)
                for c in range(KU):
                    last = act.activation(w1_g[:, c, :], w1_sb[:, c, :], ACT.Copy, scale=gl_sb[:, c:c + 1])
                last.then_inc(w1_ready, 1)

            def take_moments(chunk):
                if is_last(chunk):
                    act.wait_ge(z_last_moved, MOVES)
                else:
                    act.wait_ge(z_moved, chunk * MOVES + MOVES)
                    wait(act, o_done, chunk)
                act.copy((moment_last if is_last(chunk) else moment_cols)[:],
                         moments[:, bass.ds(chunk, 1), :, :].rearrange("p s k g -> p (s k g)")
                         ).then_inc(moments_ready, 1)

            def square_o(chunk):
                act.wait_ge(o_done, chunk + 1)
                act.activation(o_sq[:], (o_last_ps if is_last(chunk) else o_ps)[:], ACT.Square).then_inc(osq_done, 1)

            def root_o(chunk):
                act.wait_ge(ovar_done, chunk + 1)
                act.activation(o_std[:], o_var[:], ACT.Sqrt, bias=eps[:, 0:1], scale=1.0 / MAXD).then_inc(ostd_done, 1)

            def scale_o(chunk):
                act.wait_ge(orstd_done, chunk + 1)
                act.activation(o_unit[:], (o_last_ps if is_last(chunk) else o_ps)[:, 0:USED], ACT.Copy, scale=o_rstd[:, 0:1]).then_inc(o_scaled, 1)

            def save_o(chunk):
                act.wait_ge(o_turned, chunk + 1)
                act.copy(o_sb[:, :, :].rearrange("p j (s b) -> p j s b", b=P)[:, :, bass.ds(chunk, 1), :],
                         o_turn_ps[:, 0:USED].rearrange("p (j s b) -> p j s b", s=1, b=P)).then_inc(o_saved, 1)

            slots(act, [(8, in_loop(square_o)), (2, root_n), (3, square), (3, root_p), (8, in_loop(root_o)),
                        (8, in_loop(scale_o)), (0, save_cols), (3, place_x), (2, save_f), (4, save_z), (8, in_loop(save_o)),
                        (6, with_last(lambda chunk: None if is_last(chunk) else take_moments(chunk)))],
                  extra=[(1, save_xsum), (2, gain_w1), (5, save_moment_w), (5, lambda: gain_wl(0, 1)),
                         (6, lambda: gain_wl(1, 2)), (7, lambda: gain_wl(3, KZ - 3))])

            def relu_1(first, number, turn):
                for j in range(H1 // P):
                    act.wait_ge(h1_summed, H1 // P * turn + j + 1)
                    at = slice(P * first, P * (first + number))
                    act.activation(h1_sb[:, j, at], h1_dense[:, j, at], ACT.Relu,
                                   bias=b1_all[:, j:j + 1]).then_inc(h1_ready, 1)

            def relu_2(first, number, turn):
                for j in range(H2 // P):
                    act.wait_ge(h2_done, H2 // P * 2 if turn else j + 1)
                    at = slice(P * first, P * (first + number))
                    act.activation(h2_sb[:, j, at], h2_last_ps[:, P * j:P * (j + 1)] if turn else h2_ps[j][:, at], ACT.Relu, bias=b2_sb[:, j:j + 1]).then_inc(h2_ready, 1)

            square_o(CHUNKS - 2)
            root_o(CHUNKS - 2)
            scale_o(CHUNKS - 2)
            save_o(CHUNKS - 2)
            take_moments(CHUNKS - 1)
            relu_1(0, CHUNKS - 1, 0)
            square_o(CHUNKS - 1)
            root_o(CHUNKS - 1)
            scale_o(CHUNKS - 1)
            save_o(CHUNKS - 1)
            relu_1(CHUNKS - 1, 1, 1)
            relu_2(0, CHUNKS - 1, 0)
            relu_2(CHUNKS - 1, 1, 1)
            act.wait_ge(top_done, 1)
            act.copy(y_out[:], y_ps).then_inc(y_done, 1)

        @block.vector
        def _(dve):
            links = [0]

            def link(instruction):
                links[0] += 1
                instruction.then_inc(chain, 1)
                dve.wait_ge(chain, links[0])

            def centre(out, in_, mean, width):
                link(dve.tensor_reduce(mean, in_, AX.X, ALU.add))
                link(dve.tensor_scalar(mean, mean, 1.0 / width, None, ALU.mult))
                return dve.tensor_tensor(out, in_, mean.unsqueeze(2).to_broadcast(list(in_.shape)), ALU.subtract)

            dve.wait_ge(ids_in, 32)
            dve.tensor_tensor(rows_sb[:], ids_sb[:], offs_sb[:], ALU.add).then_inc(rows_ready, 1)
            dve.wait_ge(small_in, 16)
            centre(ws_c[:].unsqueeze(1), ws_sb[0:D, :].unsqueeze(1), ws_mean[:], EW).then_inc(prep_dve, 1)
            centre(wsi_c[:].unsqueeze(1), wsi_sb[0:NF, :].unsqueeze(1), wsi_mean[:], PR).then_inc(prep_dve, 1)
            dve.wait_ge(dense_in, 32)
            centre(wd_c[:], wd_sb[:], wd_mean[:], EW).then_inc(prep_dve, 1)
            dve.memset(var_n[:], 1.0)
            dve.memset(moments[PR:MOMENTS, :, :, :], 1.0)
            dve.wait_ge(mixw_in, 32)
            link(centre(row_w_sb[:], row_w_sb[:], row_w_mean[:], PR))
            wide = [P, TILES, SPAN, PR]
            dve.tensor_tensor(mixw_sb[:], row_w_sb[:].unsqueeze(2).to_broadcast(wide),
                              owner_sb[:].unsqueeze(3).to_broadcast(wide), ALU.mult).then_inc(prep_dve, 1)
            dve.wait_ge(prep_act, 7)
            link(dve.reciprocal(x_rstd[:], x_std[:]))
            link(dve.tensor_tensor(x_unit[:], proj_ps[:, 0, :], x_rstd[:], ALU.mult))
            dve.tensor_scalar(x_sb[:], x_unit[:], gd_sb[:, 0:1], bd_sb[:, 0:1], ALU.mult, ALU.add).then_inc(x_ready, 1)

            def variance_p(chunk, q):
                s = chunk * QUARTERS + q
                wait(dve, stdp_ready, s)
                for ab in range(2):
                    dve.wait_ge(sq_ready, 2 * s + ab + 1)
                    last = dve.tensor_reduce(var_p[:, QB * ab:QB * (ab + 1)], y_sq[:, QB * ab:QB * (ab + 1), :], AX.X,
                                             ALU.add)
                last.then_inc(ssq_ready, 1)

            def variance_n(chunk, q):
                t0, nt = tiles_of(q)
                s = chunk * QUARTERS + q
                dve.wait_ge(quad_done, s + 1)
                wait(dve, std_ready, s)
                dve.wait_ge(gathered[q], chunk * (32 * nt) + 32 * nt)
                dve.tensor_tensor(e_prod[:, 0:2 * nt, :].rearrange("p a d -> p (a d)"), quad_ps[:, 0:P * nt],
                                  e_rows[:, t0:t0 + nt, :].rearrange("p t d -> p (t d)"), ALU.mult).then_inc(prod_done, 1)
                dve.wait_ge(prod_done, s + 1)
                dve.tensor_reduce(var_n[:, 0:2 * nt], e_prod[:, 0:2 * nt, :], AX.X, ALU.add).then_inc(var_ready, 1)

            def norm_p(chunk, q):
                s = chunk * QUARTERS + q
                wide = [P, QB, PR]
                dve.wait_ge(stdp_ready, s + 1)
                dve.reciprocal(rstd_p[:], std_p[:]).then_inc(rstdp_done, 1)
                dve.wait_ge(rstdp_done, s + 1)
                wait(dve, dotted, s - 1)
                for ab in range(2):
                    dve.tensor_tensor(feats[:, q % 2, QB * ab:QB * (ab + 1), 2:PR + 2],
                                      proj_ps[:, ab, :].rearrange("p (b q) -> p b q", q=PR),
                                      rstd_p[:, QB * ab:QB * (ab + 1)].unsqueeze(2).to_broadcast(wide),
                                      ALU.mult).then_inc(y_ready, 1)

            def norm_n(chunk, q):
                t0, nt = tiles_of(q)
                s = chunk * QUARTERS + q
                dve.wait_ge(std_ready, s + 1)
                dve.reciprocal(rstd_n[:], std_n[:]).then_inc(rstdn_done, 1)
                dve.wait_ge(rstdn_done, s + 1)
                wait(dve, mixed, s - QUARTERS + 1 + (q < QUARTERS - 1))
                dve.tensor_tensor(e_unit[:, t0:t0 + nt, :].rearrange("p t (a d) -> p (t a) d", d=D),
                                  e_rows[:, t0:t0 + nt, :].rearrange("p t (a d) -> p (t a) d", d=D),
                                  rstd_n[:, 0:2 * nt].unsqueeze(2).to_broadcast([P, 2 * nt, D]),
                                  ALU.mult).then_inc(unit_ready, 1)

            def sum_b1():
                dve.wait_ge(bl_done, 1)
                dve.tensor_tensor(b1_all[:], bl_ps[:, 0:H1 // P], b1_sb, ALU.add).then_inc(b1_ready, 1)

            def mean_wl(first, number):
                dve.wait_ge(wl_in, 16 * 3)
                dve.tensor_reduce(wl_mean[:, first:first + number], wl_sb[:, first:first + number, :], AX.X,
                                  ALU.add).then_inc(wl_summed, 1)
                if first + number == KZ:
                    dve.wait_ge(wl_summed, 2)
                    link(dve.tensor_scalar(wl_mean[:], wl_mean[:], -1.0 / MAXD, None, ALU.mult))
                    dve.tensor_tensor(wl_bias[:], wl_mean[:], wl_gain[:], ALU.mult).then_inc(wl_mean_ready, 1)

            def choose_moments():
                dve.wait_ge(pairs_in, 16)
                shape = [P, KZ, MOMENTS]
                link(dve.tensor_tensor(pick_p[:], is_p.rearrange("p (k m) -> p k m", m=MOMENTS),
                                       bsi_c.unsqueeze(2).to_broadcast(shape), ALU.mult))
                link(dve.tensor_tensor(pick_c[:], is_c.rearrange("p (k m) -> p k m", m=MOMENTS),
                                       bsi_p.unsqueeze(2).to_broadcast(shape), ALU.mult))
                link(dve.tensor_tensor(pick[:], pick_p[:], pick_c[:], ALU.add))
                link(dve.tensor_tensor(one_w[:], bsi_p, bsi_c, ALU.mult))
                dve.tensor_scalar(pick[:, :, MOMENTS - 1], one_w[:], float(EW), None, ALU.mult).then_inc(pick_ready, 1)
                link(dve.tensor_tensor(wl_gain[:], gsi_p, gsi_c, ALU.mult))

            def centre_moment_w():
                dve.wait_ge(moment_saved, 1)
                link(dve.tensor_reduce(moment_mean[:], moment_w[:], AX.X, ALU.add))
                link(dve.tensor_scalar(moment_mean[:], moment_mean[:], 1.0 / MAXD, None, ALU.mult))
                dve.tensor_scalar(moment_w[:], moment_w[:], moment_mean[:, 0:1], None,
                                  ALU.subtract).then_inc(moment_ready, 1)

            def variance_o(chunk):
                dve.wait_ge(osq_done, chunk + 1)
                dve.tensor_reduce(o_var[:], o_sq[:], AX.X, ALU.add).then_inc(ovar_done, 1)

            def invert_o(chunk):
                dve.wait_ge(ostd_done, chunk + 1)
                dve.reciprocal(o_rstd[:], o_std[:]).then_inc(orstd_done, 1)

            slots(dve, [(2, norm_n), (8, in_loop(variance_o)), (3, variance_p), (8, in_loop(invert_o)), (3, norm_p),
                        (1, variance_n)],
                  extra=[(1, choose_moments), (1, sum_b1), (3, lambda: mean_wl(0, 3)), (4, lambda: mean_wl(3, KZ - 3)),
                         (5, centre_moment_w)])

            def add_dense(first, number, turn):
                for j in range(H1 // P):
                    dve.wait_ge(h1_done, H1 // P * turn + j + 1)
                    at = slice(P * first, P * (first + number))
                    dve.tensor_tensor(h1_dense[:, j, at], h1_ps[j][:, at], h1_dense[:, j, at],
                                      ALU.add).then_inc(h1_summed, 1)

            variance_o(CHUNKS - 2)
            invert_o(CHUNKS - 2)
            add_dense(0, CHUNKS - 1, 0)
            variance_o(CHUNKS - 1)
            invert_o(CHUNKS - 1)
            add_dense(CHUNKS - 1, 1, 1)


def kernel(**inputs):
    import concourse.bacc as bacc
    from concourse.bass_utils import run_bass_kernel_spmd

    a = {k: np.asarray(v) for k, v in inputs.items()}

    def by_partition(m):
        return np.ascontiguousarray(m.reshape(-1, P, m.shape[1]).transpose(1, 0, 2))

    def columns(v):
        return np.ascontiguousarray(v.reshape(-1, P).T)

    order = np.arange(B).reshape(CHUNKS, 2, QUARTERS, QB // 4, 4).transpose(0, 4, 2, 1, 3).reshape(-1)
    small = np.zeros((P, PACKED), np.float32)

    def put(name, v):
        begin, end = PACK[name]
        small[:v.shape[0], begin:end] = v

    put("eye", np.eye(P, dtype=np.float32))
    put("ws", np.concatenate([a["L0_rec_Ws"].T, a["L0_rec_bs"][None]]))
    put("wsi", a["L0_rec_Wsi"].T)
    put("gs", columns(a["L0_rec_gs"]))
    put("gd", columns(a["L0_rec_gd"]))
    put("bd", columns(a["L0_rec_bd"]))
    put("gl", columns(a["L0_rec_gl"][:USED]))
    put("bl", columns(a["L0_rec_bl"][:USED]))
    put("b1", columns(a["b_top1"]))
    put("b2", columns(a["b_top2"]))
    put("w3", columns(a["W_top3"][:, 0]))

    row = np.arange(TILES * P).reshape(TILES, P)
    sample, feature = row // NF, row % NF
    starts = np.concatenate([[0], np.cumsum(VOCAB)[:-1]]).astype(np.int32)
    offs = np.broadcast_to(starts[feature].T[:, None, :, None], (P, CHUNKS, TILES, 2)).reshape(P, -1)
    ids = a["ids"].reshape(CHUNKS, 2, TILES, P).transpose(3, 0, 2, 1).reshape(P, -1)
    row_w = a["L0_rec_Wsi"].T[feature].transpose(1, 0, 2)
    first = np.array([first_sample(t) for t in range(TILES)])[:, None]
    owner = ((sample - first)[:, :, None] == np.arange(SPAN)).astype(np.float32).transpose(1, 0, 2)
    p_of, c_of = np.zeros((P, KZ), int), np.zeros((P, KZ), int)
    for t, row, band, pair, number in PIECES:
        p_of[row:row + number, t] = np.arange(pair, pair + number) // BAND
        c_of[row:row + number, t] = np.arange(pair, pair + number) % BAND + BAND * band
    wl = np.zeros((P, KZ, MAXD), np.float32)
    valid = c_of <= p_of
    wl[valid] = a["L0_rec_Wl"].T[(p_of * (p_of + 1) // 2 + c_of)[valid]]
    moment_of = np.where(c_of == 0, PR, c_of - 1)
    unit = np.ones(1, np.float32)
    gains = np.concatenate([a["L0_rec_gsi"], unit, unit])
    biases = np.concatenate([a["L0_rec_bsi"], 0 * unit])
    gains_m = np.zeros((P, 1), np.float32)
    gains_m[:MOMENTS, 0] = gains
    moment = np.arange(MOMENTS)
    pairs = np.concatenate([gains[p_of], gains[moment_of], biases[p_of], biases[moment_of], gains_m,
                            (p_of[:, :, None] == moment).astype(np.float32).reshape(P, -1),
                            (moment_of[:, :, None] == moment).astype(np.float32).reshape(P, -1)], axis=1)
    w1 = a["W_top1"]
    arrays = {
        "table": np.concatenate([a[f"tbl_{n}"] for n in range(NF)]),
        "ids": np.ascontiguousarray(ids),
        "offs": np.ascontiguousarray(offs),
        "small": small,
        "row_w": np.ascontiguousarray(row_w),
        "owner": np.ascontiguousarray(owner),
        "dense_t": by_partition(np.ascontiguousarray(a["r_dense_t"][order].T)),
        "wd_t": by_partition(np.ascontiguousarray(a["L0_rec_Wd"].T)),
        "pairs": pairs,
        "wl": wl,
        "w1": by_partition(np.concatenate([w1[:USED], w1[MAXD:]])),
        "w2": by_partition(a["W_top2"]),
    }
    nc = bacc.Bacc("TRN2", target_bir_lowering=False, num_devices=1)
    args = [nc.dram_tensor(f"{name}_dram", v.shape, mybir.dt.from_np(v.dtype), kind="ExternalInput").ap()
            for name, v in arrays.items()]
    args.append(nc.dram_tensor("z_dram", (CHUNKS, BANDS, P, BAND * PR), F32).ap())
    args.append(nc.dram_tensor("s_dram", (CHUNKS, P, PR), F32).ap())
    args.append(nc.dram_tensor("out_dram", (P, CHUNKS), F32, kind="ExternalOutput").ap())
    tower(nc, *args)
    r = run_bass_kernel_spmd(nc, [{f"{name}_dram": v for name, v in arrays.items()}], core_ids=[0])
    y = np.empty((B, 1), np.float32)
    y[order, 0] = r.results[0]["out_dram"].T.reshape(-1)
    return y
```
